# Optimizing a Trainium2 kernel written in Bass

```python
import numpy as np
import jax
import jax.numpy as jnp

def _softmax(x, axis=-1):
    return jax.nn.softmax(x, axis=axis)

def _gelu(x):
    return jax.nn.gelu(x, approximate=True)

def _silu(x):
    return jax.nn.silu(x)

def _sigmoid(x):
    return jax.nn.sigmoid(x)

def _layernorm(x, axis=-1, eps=1e-05):
    m = jnp.mean(x, axis=axis, keepdims=True)
    v = jnp.var(x, axis=axis, keepdims=True)
    return (x - m) / jnp.sqrt(v + eps)

def _scatter_add(tgt, idx, src, axis=0):
    return tgt.at[idx].add(src)

def _segment_sum(src, seg, n):
    return jax.ops.segment_sum(src, seg, n)
kernel_name = 'mk_prb_d4_jaxref_r8_e15e8f'

def setup_inputs(seed: int=0):
    np.random.seed(seed)
    _w = jnp.asarray

    def _L0_attn_setup():
        import jax, jax.numpy as jnp
        import numpy as np
        D_MODEL = 128
        D_STATE = 16
        D_CONV = 4
        EXPAND = 2
        D_INNER = EXPAND * D_MODEL
        DT_RANK = (D_MODEL + 15) // 16
        B, L = (2, 128)

        def _mamba_params(key, scale=0.02):
            ks = jax.random.split(key, 6)
            return dict(inW=jax.random.normal(ks[0], (2 * D_INNER, D_MODEL), jnp.float32) * scale, convW=jax.random.normal(ks[1], (D_INNER, 1, D_CONV), jnp.float32) * scale, convb=jnp.zeros((D_INNER,), jnp.float32), xprojW=jax.random.normal(ks[2], (DT_RANK + 2 * D_STATE, D_INNER), jnp.float32) * scale, dtW=jax.random.normal(ks[3], (D_INNER, DT_RANK), jnp.float32) * scale, dtb=jax.random.normal(ks[4], (D_INNER,), jnp.float32) * scale, A_log=jnp.log(jnp.tile(jnp.arange(1, D_STATE + 1, dtype=jnp.float32), (D_INNER, 1))), Dskip=jnp.ones((D_INNER,), jnp.float32), outW=jax.random.normal(ks[5], (D_MODEL, D_INNER), jnp.float32) * scale)

        def _layernorm(x, w, b, eps=1e-05):
            mu = jnp.mean(x, axis=-1, keepdims=True)
            var = jnp.var(x, axis=-1, keepdims=True)
            return (x - mu) * jax.lax.rsqrt(var + eps) * w + b

        def _mamba(x, inW, convW, convb, xprojW, dtW, dtb, A_log, Dskip, outW):
            xz = jnp.einsum('bld,ed->ble', x, inW)
            xs, z = jnp.split(xz, 2, axis=-1)
            xc = jnp.transpose(xs, (0, 2, 1))
            xc = jax.lax.conv_general_dilated(xc, convW, window_strides=(1,), padding=[(D_CONV - 1, 0)], feature_group_count=D_INNER)
            xs = jax.nn.silu(jnp.transpose(xc + convb[None, :, None], (0, 2, 1)))
            xdb = jnp.einsum('bld,ed->ble', xs, xprojW)
            dt, Bm, Cm = jnp.split(xdb, [DT_RANK, DT_RANK + D_STATE], axis=-1)
            dt = jax.nn.softplus(jnp.einsum('blr,dr->bld', dt, dtW) + dtb)
            A = -jnp.exp(A_log)
            dA = jnp.exp(dt[..., None] * A)
            dBx = dt[..., None] * Bm[:, :, None, :] * xs[..., None]

            def step(h, inputs):
                dA_t, dBx_t, C_t = inputs
                h = h * dA_t + dBx_t
                y = jnp.einsum('bds,bs->bd', h, C_t)
                return (h, y)
            h0 = jnp.zeros((x.shape[0], D_INNER, D_STATE), x.dtype)
            _, ys = jax.lax.scan(step, h0, (jnp.moveaxis(dA, 1, 0), jnp.moveaxis(dBx, 1, 0), jnp.moveaxis(Cm, 1, 0)))
            y = jnp.moveaxis(ys, 0, 1)
            y = (y + xs * Dskip) * jax.nn.silu(z)
            return jnp.einsum('bld,ed->ble', y, outW)
        key = jax.random.key(seed)
        kx, kf, kb, kp = jax.random.split(key, 4)
        inp = {'x': jax.random.normal(kx, (B, L, D_MODEL), jnp.float32)}
        inp['ln_w'] = jnp.ones((D_MODEL,), jnp.float32)
        inp['ln_b'] = jnp.zeros((D_MODEL,), jnp.float32)
        for pref, k in (('f_', kf), ('b_', kb)):
            for name, v in _mamba_params(k).items():
                inp[pref + name] = v
        inp['proj_W'] = jax.random.normal(kp, (D_MODEL, 2 * D_MODEL), jnp.float32) * 0.02
        inp['proj_b'] = jnp.zeros((D_MODEL,), jnp.float32)
        return inp
    _L0_attn_in = _L0_attn_setup()

    def _L0_ffn_setup():
        import jax, jax.numpy as jnp
        import numpy as np
        TOP_K = 2
        key = jax.random.key(seed)
        k1, k2, k3 = jax.random.split(key, 3)
        B, S, D, E = (8, 256, 128, 8)
        x = jax.random.normal(k1, (B, S, D), dtype=jnp.float32)
        gate_w = jax.random.normal(k2, (E, D), dtype=jnp.float32) * (1.0 / np.sqrt(D))
        gate_b = jnp.zeros((E,), dtype=jnp.float32)
        expert_w = jax.random.normal(k3, (E, D, D), dtype=jnp.float32) * (1.0 / np.sqrt(D))
        expert_b = jnp.zeros((E, D), dtype=jnp.float32)
        return {'x': x, 'gate_w': gate_w, 'gate_b': gate_b, 'expert_w': expert_w, 'expert_b': expert_b}
    _L0_ffn_in = _L0_ffn_setup()

    def _L1_attn_setup():
        import jax, jax.numpy as jnp
        import numpy as np
        S, B, E, H = (256, 2, 128, 16)
        D = E // H

        def ste_sign(x):
            return jax.lax.stop_gradient(jnp.sign(x) - x) + x

        def ste_binarize01(x):
            return jax.lax.stop_gradient((x > 0).astype(x.dtype) - x) + x
        key = jax.random.key(seed)
        ks = jax.random.split(key, 5)
        query = jax.random.normal(ks[0], (S, B, E), dtype=jnp.float32)
        mk = lambda k: (jax.random.uniform(k, (E,), dtype=jnp.float32) * 2.0 - 1.0) * 0.001
        return {'query': query, 'w_q': mk(ks[1]), 'w_k': mk(ks[2]), 'w_v': mk(ks[3]), 'w_o': mk(ks[4])}
    _L1_attn_in = _L1_attn_setup()

    def _L1_ffn_setup():
        import jax, jax.numpy as jnp
        import numpy as np
        NUM_LOCAL_EXPERTS = 8
        D_MODEL = 128
        D_FF = 512
        B, EC = (4, NUM_LOCAL_EXPERTS * 128)
        key = jax.random.key(seed)
        k_in, k_w1, k_w2 = jax.random.split(key, 3)
        s1 = 1.0 / np.sqrt(D_MODEL)
        s2 = 1.0 / np.sqrt(D_FF)
        return {'inputs': jax.random.normal(k_in, (B, EC, D_MODEL), dtype=jnp.float32), 'w1': jax.random.normal(k_w1, (NUM_LOCAL_EXPERTS, D_FF, D_MODEL), dtype=jnp.float32) * s1, 'b1': jnp.zeros((NUM_LOCAL_EXPERTS, D_FF), dtype=jnp.float32), 'w2': jax.random.normal(k_w2, (NUM_LOCAL_EXPERTS, D_MODEL, D_FF), dtype=jnp.float32) * s2, 'b2': jnp.zeros((NUM_LOCAL_EXPERTS, D_MODEL), dtype=jnp.float32)}
    _L1_ffn_in = _L1_ffn_setup()

    def _L2_attn_setup():
        import jax, jax.numpy as jnp
        import numpy as np
        import math
        D_MODEL = 128
        D_STATE = 128
        EXPAND = 2
        HEADDIM = 64
        NGROUPS = 1
        D_INNER = EXPAND * D_MODEL
        NHEADS = D_INNER // HEADDIM
        ROPE_FRACTION = 0.5
        SPLIT = int(D_STATE * ROPE_FRACTION)
        SPLIT -= SPLIT % 2
        NUM_ANGLES = SPLIT // 2
        A_FLOOR = 0.0001
        EPS = 1e-05
        DT_MIN, DT_MAX, DT_INIT_FLOOR = (0.001, 0.1, 0.0001)
        D_IN_PROJ = 2 * D_INNER + 2 * D_STATE * NGROUPS + 3 * NHEADS + NUM_ANGLES

        def _rmsnorm(x, w):
            xf = x.astype(jnp.float32)
            return xf * jax.lax.rsqrt(jnp.mean(xf * xf, axis=-1, keepdims=True) + EPS) * w

        def _rope(v, theta):
            v1 = v[..., :NUM_ANGLES]
            v2 = v[..., NUM_ANGLES:SPLIT]
            rest = v[..., SPLIT:]
            c, s = (jnp.cos(theta), jnp.sin(theta))
            return jnp.concatenate([v1 * c - v2 * s, v1 * s + v2 * c, rest], axis=-1)
        key = jax.random.key(seed)
        ks = jax.random.split(key, 6)
        b, l = (2, 128)
        u = jax.random.normal(ks[0], (b, l, D_MODEL), jnp.float32)
        W_in = jax.random.normal(ks[1], (D_IN_PROJ, D_MODEL), jnp.float32) * 0.02
        W_out = jax.random.normal(ks[2], (D_MODEL, D_INNER), jnp.float32) * 0.02
        _dt = jnp.exp(jax.random.uniform(ks[3], (NHEADS,), jnp.float32) * (math.log(DT_MAX) - math.log(DT_MIN)) + math.log(DT_MIN))
        _dt = jnp.clip(_dt, DT_INIT_FLOOR, None)
        dt_bias = _dt + jnp.log(-jnp.expm1(-_dt))
        B_bias = jnp.ones((NHEADS, D_STATE), jnp.float32)
        C_bias = jnp.ones((NHEADS, D_STATE), jnp.float32)
        B_norm_w = jnp.ones((D_STATE,), jnp.float32)
        C_norm_w = jnp.ones((D_STATE,), jnp.float32)
        D_param = jnp.ones((NHEADS,), jnp.float32)
        return {'u': u, 'W_in': W_in, 'W_out': W_out, 'dt_bias': dt_bias, 'B_bias': B_bias, 'C_bias': C_bias, 'B_norm_w': B_norm_w, 'C_norm_w': C_norm_w, 'D_param': D_param}
    _L2_attn_in = _L2_attn_setup()

    def _L2_ffn_setup():
        import jax, jax.numpy as jnp
        import numpy as np
        THRESH_FACTOR = 0.7

        def ternary_quantize(w):
            delta = THRESH_FACTOR * jnp.mean(jnp.abs(w))
            return jnp.where(w > delta, 1.0, jnp.where(w < -delta, -1.0, 0.0)).astype(w.dtype)
        key = jax.random.key(seed)
        k1, k2, k3 = jax.random.split(key, 3)
        B, S, D_IN, D_OUT = (8, 512, 128, 128)
        inp = {'input': jax.random.normal(k1, (B, S, D_IN), dtype=jnp.float32), 'weight': jax.random.normal(k2, (D_OUT, D_IN), dtype=jnp.float32) * (1.0 / np.sqrt(D_IN)), 'alpha': jnp.ones((1,), dtype=jnp.float32), 'bias': jax.random.normal(k3, (D_OUT,), dtype=jnp.float32) * (1.0 / np.sqrt(D_IN))}
        return inp
    _L2_ffn_in = _L2_ffn_setup()

    def _L3_attn_setup():
        import jax, jax.numpy as jnp
        import numpy as np
        B, S, D, H = (2, 256, 128, 16)
        HD = D // H
        key = jax.random.key(seed)
        k1, k2, k3, k4, k5 = jax.random.split(key, 5)
        scale = 1.0 / np.sqrt(D)
        return {'x': jax.random.normal(k1, (B, S, D), dtype=jnp.float32), 'W_qkv': jax.random.normal(k2, (D, 3 * D), dtype=jnp.float32) * scale, 'b_qkv': jax.random.normal(k3, (3 * D,), dtype=jnp.float32) * 0.01, 'W_out': jax.random.normal(k4, (D, D), dtype=jnp.float32) * scale, 'b_out': jax.random.normal(k5, (D,), dtype=jnp.float32) * 0.01}
    _L3_attn_in = _L3_attn_setup()

    def _L3_ffn_setup():
        import jax, jax.numpy as jnp
        import numpy as np
        N_EMBD = 128
        NUM_EXPERTS = 8
        TOP_K = 2

        def new_gelu(x):
            c = jnp.sqrt(2.0 / jnp.pi).astype(x.dtype)
            return 0.5 * x * (1.0 + jnp.tanh(c * (x + 0.044715 * x ** 3)))
        key = jax.random.key(seed)
        ks = jax.random.split(key, 6)
        C, E, H = (N_EMBD, NUM_EXPERTS, 4 * N_EMBD)
        x = jax.random.normal(ks[0], (4, 256, C), dtype=jnp.float32)
        router_w = 0.02 * jax.random.normal(ks[1], (E, C), dtype=jnp.float32)
        w1 = 0.02 * jax.random.normal(ks[2], (E, H, C), dtype=jnp.float32)
        b1 = jnp.zeros((E, H), dtype=jnp.float32)
        w2 = 0.02 * jax.random.normal(ks[3], (E, C, H), dtype=jnp.float32)
        b2 = jnp.zeros((E, C), dtype=jnp.float32)
        return {'x': x, 'router_w': router_w, 'w1': w1, 'b1': b1, 'w2': w2, 'b2': b2}
    _L3_ffn_in = _L3_ffn_setup()
    _d = {'L0_attn_x': _L0_attn_in['x'], 'L0_attn_ln_w': _L0_attn_in['ln_w'], 'L0_attn_ln_b': _L0_attn_in['ln_b'], 'L0_attn_f_inW': _L0_attn_in['f_inW'], 'L0_attn_f_convW': _L0_attn_in['f_convW'], 'L0_attn_f_convb': _L0_attn_in['f_convb'], 'L0_attn_f_xprojW': _L0_attn_in['f_xprojW'], 'L0_attn_f_dtW': _L0_attn_in['f_dtW'], 'L0_attn_f_dtb': _L0_attn_in['f_dtb'], 'L0_attn_f_A_log': _L0_attn_in['f_A_log'], 'L0_attn_f_Dskip': _L0_attn_in['f_Dskip'], 'L0_attn_f_outW': _L0_attn_in['f_outW'], 'L0_attn_b_inW': _L0_attn_in['b_inW'], 'L0_attn_b_convW': _L0_attn_in['b_convW'], 'L0_attn_b_convb': _L0_attn_in['b_convb'], 'L0_attn_b_xprojW': _L0_attn_in['b_xprojW'], 'L0_attn_b_dtW': _L0_attn_in['b_dtW'], 'L0_attn_b_dtb': _L0_attn_in['b_dtb'], 'L0_attn_b_A_log': _L0_attn_in['b_A_log'], 'L0_attn_b_Dskip': _L0_attn_in['b_Dskip'], 'L0_attn_b_outW': _L0_attn_in['b_outW'], 'L0_attn_proj_W': _L0_attn_in['proj_W'], 'L0_attn_proj_b': _L0_attn_in['proj_b'], 'L0_ffn_gate_w': _L0_ffn_in['gate_w'], 'L0_ffn_gate_b': _L0_ffn_in['gate_b'], 'L0_ffn_expert_w': _L0_ffn_in['expert_w'], 'L0_ffn_expert_b': _L0_ffn_in['expert_b'], 'L1_attn_w_q': _L1_attn_in['w_q'], 'L1_attn_w_k': _L1_attn_in['w_k'], 'L1_attn_w_v': _L1_attn_in['w_v'], 'L1_attn_w_o': _L1_attn_in['w_o'], 'L1_ffn_w1': _L1_ffn_in['w1'], 'L1_ffn_b1': _L1_ffn_in['b1'], 'L1_ffn_w2': _L1_ffn_in['w2'], 'L1_ffn_b2': _L1_ffn_in['b2'], 'L2_attn_W_in': _L2_attn_in['W_in'], 'L2_attn_W_out': _L2_attn_in['W_out'], 'L2_attn_dt_bias': _L2_attn_in['dt_bias'], 'L2_attn_B_bias': _L2_attn_in['B_bias'], 'L2_attn_C_bias': _L2_attn_in['C_bias'], 'L2_attn_B_norm_w': _L2_attn_in['B_norm_w'], 'L2_attn_C_norm_w': _L2_attn_in['C_norm_w'], 'L2_attn_D_param': _L2_attn_in['D_param'], 'L2_ffn_weight': _L2_ffn_in['weight'], 'L2_ffn_alpha': _L2_ffn_in['alpha'], 'L2_ffn_bias': _L2_ffn_in['bias'], 'L3_attn_W_qkv': _L3_attn_in['W_qkv'], 'L3_attn_b_qkv': _L3_attn_in['b_qkv'], 'L3_attn_W_out': _L3_attn_in['W_out'], 'L3_attn_b_out': _L3_attn_in['b_out'], 'L3_ffn_router_w': _L3_ffn_in['router_w'], 'L3_ffn_w1': _L3_ffn_in['w1'], 'L3_ffn_b1': _L3_ffn_in['b1'], 'L3_ffn_w2': _L3_ffn_in['w2'], 'L3_ffn_b2': _L3_ffn_in['b2']}
    _x0 = _d['L0_attn_x']
    _d['L0_attn_x'] = jax.random.normal(jax.random.fold_in(jax.random.key(seed), 1), (4, 1024, 128), dtype=_x0.dtype)
    del _x0
    return _d

def reference(L0_attn_x, L0_attn_ln_w, L0_attn_ln_b, L0_attn_f_inW, L0_attn_f_convW, L0_attn_f_convb, L0_attn_f_xprojW, L0_attn_f_dtW, L0_attn_f_dtb, L0_attn_f_A_log, L0_attn_f_Dskip, L0_attn_f_outW, L0_attn_b_inW, L0_attn_b_convW, L0_attn_b_convb, L0_attn_b_xprojW, L0_attn_b_dtW, L0_attn_b_dtb, L0_attn_b_A_log, L0_attn_b_Dskip, L0_attn_b_outW, L0_attn_proj_W, L0_attn_proj_b, L0_ffn_gate_w, L0_ffn_gate_b, L0_ffn_expert_w, L0_ffn_expert_b, L1_attn_w_q, L1_attn_w_k, L1_attn_w_v, L1_attn_w_o, L1_ffn_w1, L1_ffn_b1, L1_ffn_w2, L1_ffn_b2, L2_attn_W_in, L2_attn_W_out, L2_attn_dt_bias, L2_attn_B_bias, L2_attn_C_bias, L2_attn_B_norm_w, L2_attn_C_norm_w, L2_attn_D_param, L2_ffn_weight, L2_ffn_alpha, L2_ffn_bias, L3_attn_W_qkv, L3_attn_b_qkv, L3_attn_W_out, L3_attn_b_out, L3_ffn_router_w, L3_ffn_w1, L3_ffn_b1, L3_ffn_w2, L3_ffn_b2):

    def _L0_attn_ref(x, ln_w, ln_b, f_inW, f_convW, f_convb, f_xprojW, f_dtW, f_dtb, f_A_log, f_Dskip, f_outW, b_inW, b_convW, b_convb, b_xprojW, b_dtW, b_dtb, b_A_log, b_Dskip, b_outW, proj_W, proj_b):
        import jax, jax.numpy as jnp
        import numpy as np
        D_MODEL = 128
        D_STATE = 16
        D_CONV = 4
        EXPAND = 2
        D_INNER = EXPAND * D_MODEL
        DT_RANK = (D_MODEL + 15) // 16
        B, L = (2, 128)

        def _mamba_params(key, scale=0.02):
            ks = jax.random.split(key, 6)
            return dict(inW=jax.random.normal(ks[0], (2 * D_INNER, D_MODEL), jnp.float32) * scale, convW=jax.random.normal(ks[1], (D_INNER, 1, D_CONV), jnp.float32) * scale, convb=jnp.zeros((D_INNER,), jnp.float32), xprojW=jax.random.normal(ks[2], (DT_RANK + 2 * D_STATE, D_INNER), jnp.float32) * scale, dtW=jax.random.normal(ks[3], (D_INNER, DT_RANK), jnp.float32) * scale, dtb=jax.random.normal(ks[4], (D_INNER,), jnp.float32) * scale, A_log=jnp.log(jnp.tile(jnp.arange(1, D_STATE + 1, dtype=jnp.float32), (D_INNER, 1))), Dskip=jnp.ones((D_INNER,), jnp.float32), outW=jax.random.normal(ks[5], (D_MODEL, D_INNER), jnp.float32) * scale)

        def _layernorm(x, w, b, eps=1e-05):
            mu = jnp.mean(x, axis=-1, keepdims=True)
            var = jnp.var(x, axis=-1, keepdims=True)
            return (x - mu) * jax.lax.rsqrt(var + eps) * w + b

        def _mamba(x, inW, convW, convb, xprojW, dtW, dtb, A_log, Dskip, outW):
            xz = jnp.einsum('bld,ed->ble', x, inW)
            xs, z = jnp.split(xz, 2, axis=-1)
            xc = jnp.transpose(xs, (0, 2, 1))
            xc = jax.lax.conv_general_dilated(xc, convW, window_strides=(1,), padding=[(D_CONV - 1, 0)], feature_group_count=D_INNER)
            xs = jax.nn.silu(jnp.transpose(xc + convb[None, :, None], (0, 2, 1)))
            xdb = jnp.einsum('bld,ed->ble', xs, xprojW)
            dt, Bm, Cm = jnp.split(xdb, [DT_RANK, DT_RANK + D_STATE], axis=-1)
            dt = jax.nn.softplus(jnp.einsum('blr,dr->bld', dt, dtW) + dtb)
            A = -jnp.exp(A_log)
            dA = jnp.exp(dt[..., None] * A)
            dBx = dt[..., None] * Bm[:, :, None, :] * xs[..., None]

            def step(h, inputs):
                dA_t, dBx_t, C_t = inputs
                h = h * dA_t + dBx_t
                y = jnp.einsum('bds,bs->bd', h, C_t)
                return (h, y)
            h0 = jnp.zeros((x.shape[0], D_INNER, D_STATE), x.dtype)
            _, ys = jax.lax.scan(step, h0, (jnp.moveaxis(dA, 1, 0), jnp.moveaxis(dBx, 1, 0), jnp.moveaxis(Cm, 1, 0)))
            y = jnp.moveaxis(ys, 0, 1)
            y = (y + xs * Dskip) * jax.nn.silu(z)
            return jnp.einsum('bld,ed->ble', y, outW)
        normed = _layernorm(x, ln_w, ln_b)
        fwd_out = _mamba(normed, f_inW, f_convW, f_convb, f_xprojW, f_dtW, f_dtb, f_A_log, f_Dskip, f_outW)
        bwd_out = _mamba(normed[:, ::-1, :], b_inW, b_convW, b_convb, b_xprojW, b_dtW, b_dtb, b_A_log, b_Dskip, b_outW)[:, ::-1, :]
        combined = jnp.concatenate([fwd_out, bwd_out], axis=-1)
        return x + jnp.einsum('blc,ec->ble', combined, proj_W) + proj_b

    def _L0_ffn_ref(x, gate_w, gate_b, expert_w, expert_b):
        import jax, jax.numpy as jnp
        import numpy as np
        TOP_K = 2
        gate = jnp.einsum('bsd,ed->bse', x, gate_w) + gate_b
        _, idx = jax.lax.top_k(gate, TOP_K)
        E = gate_w.shape[0]
        flat_idx = idx.reshape(-1)
        counts = jnp.zeros((E,), dtype=x.dtype).at[flat_idx].add(1.0)
        expert_out = jax.nn.relu(jnp.einsum('bsd,ehd->bseh', x, expert_w) + expert_b)
        total = flat_idx.size
        out = jnp.einsum('bseh,e->bsh', expert_out, counts) / total
        return out

    def _L1_attn_ref(query, w_q, w_k, w_v, w_o):
        import jax, jax.numpy as jnp
        import numpy as np
        S, B, E, H = (256, 2, 128, 16)
        D = E // H

        def ste_sign(x):
            return jax.lax.stop_gradient(jnp.sign(x) - x) + x

        def ste_binarize01(x):
            return jax.lax.stop_gradient((x > 0).astype(x.dtype) - x) + x
        S_, B_, E_ = query.shape
        q = query * ste_sign(w_q)
        k = query * ste_sign(w_k)
        v = query * ste_sign(w_v)

        def to_heads(x):
            return x.reshape(S_, B_ * H, D).transpose(1, 0, 2)
        q, k, v = (to_heads(q), to_heads(k), to_heads(v))
        q = q / jnp.sqrt(jnp.asarray(D, q.dtype))
        attn = jnp.einsum('bnd,bmd->bnm', q, k)
        attn = ste_binarize01(attn)
        out = jnp.einsum('bnm,bmd->bnd', attn, v)
        out = out.transpose(1, 0, 2).reshape(S_, B_, E_)
        out = ste_sign(out) * ste_sign(w_o)
        return out

    def _L1_ffn_ref(inputs, w1, b1, w2, b2):
        import jax, jax.numpy as jnp
        import numpy as np
        NUM_LOCAL_EXPERTS = 8
        D_MODEL = 128
        D_FF = 512
        B, EC = (4, NUM_LOCAL_EXPERTS * 128)
        B_, EC_, D = inputs.shape
        E = w1.shape[0]
        C = EC_ // E
        x = inputs.reshape(B_, E, C, D)
        h = jnp.einsum('becd,efd->becf', x, w1) + b1[None, :, None, :]
        h = jax.nn.gelu(h, approximate=False)
        y = jnp.einsum('becf,edf->becd', h, w2) + b2[None, :, None, :]
        return y.reshape(B_, EC_, D)

    def _L2_attn_ref(u, W_in, W_out, dt_bias, B_bias, C_bias, B_norm_w, C_norm_w, D_param):
        import jax, jax.numpy as jnp
        import numpy as np
        import math
        D_MODEL = 128
        D_STATE = 128
        EXPAND = 2
        HEADDIM = 64
        NGROUPS = 1
        D_INNER = EXPAND * D_MODEL
        NHEADS = D_INNER // HEADDIM
        ROPE_FRACTION = 0.5
        SPLIT = int(D_STATE * ROPE_FRACTION)
        SPLIT -= SPLIT % 2
        NUM_ANGLES = SPLIT // 2
        A_FLOOR = 0.0001
        EPS = 1e-05
        DT_MIN, DT_MAX, DT_INIT_FLOOR = (0.001, 0.1, 0.0001)
        D_IN_PROJ = 2 * D_INNER + 2 * D_STATE * NGROUPS + 3 * NHEADS + NUM_ANGLES

        def _rmsnorm(x, w):
            xf = x.astype(jnp.float32)
            return xf * jax.lax.rsqrt(jnp.mean(xf * xf, axis=-1, keepdims=True) + EPS) * w

        def _rope(v, theta):
            v1 = v[..., :NUM_ANGLES]
            v2 = v[..., NUM_ANGLES:SPLIT]
            rest = v[..., SPLIT:]
            c, s = (jnp.cos(theta), jnp.sin(theta))
            return jnp.concatenate([v1 * c - v2 * s, v1 * s + v2 * c, rest], axis=-1)
        b, l, _ = u.shape
        proj = u @ W_in.T
        sizes = [D_INNER, D_INNER, D_STATE * NGROUPS, D_STATE * NGROUPS, NHEADS, NHEADS, NHEADS, NUM_ANGLES]
        splits = np.cumsum(sizes)[:-1]
        z, x, B, C, dd_dt, dd_A, trap, angles = jnp.split(proj, splits, axis=-1)
        z = z.reshape(b, l, NHEADS, HEADDIM)
        x = x.reshape(b, l, NHEADS, HEADDIM)
        B = B.reshape(b, l, NGROUPS, D_STATE)
        C = C.reshape(b, l, NGROUPS, D_STATE)
        a = -jax.nn.softplus(dd_A.astype(jnp.float32))
        a = jnp.minimum(a, -A_FLOOR)
        dt = jax.nn.softplus(dd_dt.astype(jnp.float32) + dt_bias)
        adt = a * dt
        theta = jnp.cumsum(angles[:, :, None, :].astype(jnp.float32) * dt[..., None], axis=1)
        Bn = _rmsnorm(B, B_norm_w)
        Cn = _rmsnorm(C, C_norm_w)
        head_group = np.repeat(np.arange(NGROUPS), NHEADS // NGROUPS)
        Bh = Bn[:, :, head_group, :] + B_bias
        Ch = Cn[:, :, head_group, :] + C_bias
        Bh = _rope(Bh, theta)
        Ch = _rope(Ch, theta)
        lam = jax.nn.sigmoid(trap.astype(jnp.float32))
        g = jnp.exp(adt)
        xs = (jnp.moveaxis(x.astype(jnp.float32), 1, 0), jnp.moveaxis(Bh, 1, 0), jnp.moveaxis(Ch, 1, 0), jnp.moveaxis(dt, 1, 0), jnp.moveaxis(g, 1, 0), jnp.moveaxis(lam, 1, 0))
        h0 = jnp.zeros((b, NHEADS, HEADDIM, D_STATE), jnp.float32)
        bx0 = jnp.zeros_like(h0)

        def step(carry, inp):
            h, bx_prev = carry
            x_t, B_t, C_t, dt_t, g_t, lam_t = inp
            bx_t = x_t[..., :, None] * B_t[..., None, :]
            ge = g_t[..., None, None]
            dte = dt_t[..., None, None]
            le = lam_t[..., None, None]
            h = ge * h + dte * (le * bx_t + (1.0 - le) * ge * bx_prev)
            y_t = jnp.einsum('bhpn,bhn->bhp', h, C_t)
            return ((h, bx_t), y_t)
        _, ys = jax.lax.scan(step, (h0, bx0), xs)
        y = jnp.moveaxis(ys, 0, 1) + D_param[:, None] * x
        y = y * jax.nn.silu(z)
        y = y.reshape(b, l, D_INNER).astype(u.dtype)
        return y @ W_out.T

    def _L2_ffn_ref(input, weight, alpha, bias):
        import jax, jax.numpy as jnp
        import numpy as np
        THRESH_FACTOR = 0.7

        def ternary_quantize(w):
            delta = THRESH_FACTOR * jnp.mean(jnp.abs(w))
            return jnp.where(w > delta, 1.0, jnp.where(w < -delta, -1.0, 0.0)).astype(w.dtype)
        w_ternary = ternary_quantize(weight)
        w_eff = w_ternary * alpha
        out = jnp.einsum('bsd,od->bso', input, w_eff) + bias
        return out

    def _L3_attn_ref(x, W_qkv, b_qkv, W_out, b_out):
        import jax, jax.numpy as jnp
        import numpy as np
        B, S, D, H = (2, 256, 128, 16)
        HD = D // H
        b, s, d = x.shape
        h, hd = (H, HD)
        qkv = (x @ W_qkv + b_qkv).reshape(b, s, h, 3 * hd)
        q = qkv[..., :hd]
        k = qkv[..., hd:2 * hd]
        v = qkv[..., 2 * hd:]
        logits = jnp.einsum('bshd,bkhd->bhsk', q, k) / np.sqrt(hd)
        q_pos = jnp.arange(s)[:, None]
        k_pos = jnp.arange(s)[None, :]
        mask = k_pos > q_pos
        logits = jnp.where(mask[None, None, :, :], -jnp.inf, logits)
        attn = jax.nn.softmax(logits, axis=-1)
        out = jnp.einsum('bhsk,bkhd->bshd', attn, v).reshape(b, s, d)
        return out @ W_out + b_out

    def _L3_ffn_ref(x, router_w, w1, b1, w2, b2):
        import jax, jax.numpy as jnp
        import numpy as np
        N_EMBD = 128
        NUM_EXPERTS = 8
        TOP_K = 2

        def new_gelu(x):
            c = jnp.sqrt(2.0 / jnp.pi).astype(x.dtype)
            return 0.5 * x * (1.0 + jnp.tanh(c * (x + 0.044715 * x ** 3)))
        B, T, C = x.shape
        E = router_w.shape[0]
        x_flat = x.reshape(B * T, C)
        router_logits = x_flat @ router_w.T
        router_probs = jax.nn.softmax(router_logits, axis=-1)
        top_k_probs, top_k_idx = jax.lax.top_k(router_probs, TOP_K)
        top_k_probs = top_k_probs / (top_k_probs.sum(axis=-1, keepdims=True) + 1e-08)
        cw = (jax.nn.one_hot(top_k_idx, E, dtype=x.dtype) * top_k_probs[..., None]).sum(axis=1)
        output = jnp.zeros_like(x_flat)
        for e in range(E):
            h = new_gelu(x_flat @ w1[e].T + b1[e])
            out_e = h @ w2[e].T + b2[e]
            output = output + cw[:, e:e + 1] * out_e
        return output.reshape(B, T, C)
    x = L0_attn_x
    xn = _layernorm(x, axis=-1)
    x = x + _L0_attn_ref(xn, L0_attn_ln_w, L0_attn_ln_b, L0_attn_f_inW, L0_attn_f_convW, L0_attn_f_convb, L0_attn_f_xprojW, L0_attn_f_dtW, L0_attn_f_dtb, L0_attn_f_A_log, L0_attn_f_Dskip, L0_attn_f_outW, L0_attn_b_inW, L0_attn_b_convW, L0_attn_b_convb, L0_attn_b_xprojW, L0_attn_b_dtW, L0_attn_b_dtb, L0_attn_b_A_log, L0_attn_b_Dskip, L0_attn_b_outW, L0_attn_proj_W, L0_attn_proj_b) + _L0_ffn_ref(xn, L0_ffn_gate_w, L0_ffn_gate_b, L0_ffn_expert_w, L0_ffn_expert_b)
    xn = _layernorm(x, axis=-1)
    x = x + _L1_attn_ref(xn, L1_attn_w_q, L1_attn_w_k, L1_attn_w_v, L1_attn_w_o) + _L1_ffn_ref(xn, L1_ffn_w1, L1_ffn_b1, L1_ffn_w2, L1_ffn_b2)
    xn = _layernorm(x, axis=-1)
    x = x + _L2_attn_ref(xn, L2_attn_W_in, L2_attn_W_out, L2_attn_dt_bias, L2_attn_B_bias, L2_attn_C_bias, L2_attn_B_norm_w, L2_attn_C_norm_w, L2_attn_D_param) + _L2_ffn_ref(xn, L2_ffn_weight, L2_ffn_alpha, L2_ffn_bias)
    xn = _layernorm(x, axis=-1)
    x = x + _L3_attn_ref(xn, L3_attn_W_qkv, L3_attn_b_qkv, L3_attn_W_out, L3_attn_b_out) + _L3_ffn_ref(xn, L3_ffn_router_w, L3_ffn_w1, L3_ffn_b1, L3_ffn_w2, L3_ffn_b2)
    return x

_drawn_inputs = setup_inputs


def setup_inputs(seed=0):
    import zlib

    import numpy as np

    out = dict(_drawn_inputs(seed))
    spreads = {'L0_attn_ln_w': (1.0, 0.6),
     'L0_attn_ln_b': (0.0, 0.8),
     'L0_attn_f_convb': (0.0, 0.8),
     'L0_attn_f_Dskip': (1.0, 0.6),
     'L0_attn_b_convb': (0.0, 0.8),
     'L0_attn_b_Dskip': (1.0, 0.6),
     'L0_attn_proj_b': (0.0, 0.8),
     'L0_ffn_gate_b': (0.0, 2.0),
     'L0_ffn_expert_b': (0.0, 2.0),
     'L1_ffn_b1': (0.0, 2.0),
     'L1_ffn_b2': (0.0, 0.8),
     'L2_attn_B_bias': (1.0, 0.6),
     'L2_attn_C_bias': (1.0, 0.6),
     'L2_attn_B_norm_w': (1.0, 0.6),
     'L2_attn_C_norm_w': (1.0, 0.6),
     'L2_attn_D_param': (1.0, 0.6),
     'L3_ffn_b1': (0.0, 0.8),
     'L3_ffn_b2': (0.0, 2.0)}
    factors = {'L0_attn_f_inW': 6.485,
     'L0_attn_f_convW': 8.0,
     'L0_attn_f_xprojW': 8.0,
     'L0_attn_f_dtW': 8.0,
     'L0_attn_f_dtb': 8.0,
     'L0_attn_f_A_log': 8.0,
     'L0_attn_f_outW': 7.012,
     'L0_attn_b_inW': 6.047,
     'L0_attn_b_convW': 8.0,
     'L0_attn_b_xprojW': 8.0,
     'L0_attn_b_dtW': 8.0,
     'L0_attn_b_dtb': 8.0,
     'L0_attn_b_A_log': 8.0,
     'L0_attn_b_outW': 6.64,
     'L0_attn_proj_W': 5.931,
     'L2_attn_dt_bias': 21.976,
     'L2_ffn_bias': 17.274,
     'L3_attn_W_qkv': 2.712,
     'L3_attn_b_qkv': 39.246,
     'L3_attn_W_out': 2.682,
     'L3_attn_b_out': 200.0,
     'L3_ffn_router_w': 7.166,
     'L3_ffn_w1': 8.0,
     'L3_ffn_w2': 8.0,
     'L0_ffn_gate_w': 57.738,
     'L0_ffn_expert_w': 4.572,
     'L2_attn_W_in': 8.0,
     'L2_attn_W_out': 8.0}
    for name, (base, spread) in spreads.items():
        noise = np.random.default_rng([zlib.crc32(name.encode()), seed]).standard_normal(out[name].shape)
        drawn = base * np.exp(spread * noise) if base else spread * noise
        out[name] = jnp.asarray(drawn.astype(out[name].dtype))
    for name, factor in factors.items():
        out[name] = (out[name] * factor).astype(out[name].dtype)
    return out
```

```python
from contextlib import ExitStack

import numpy as np

import concourse.bass as bass
from concourse import mybir
from concourse.alu_op_type import AluOpType as ALU

ACT = mybir.ActivationFunctionType
F32 = mybir.dt.float32
BF16 = mybir.dt.bfloat16
AX_X = mybir.AxisListType.X
ds = bass.ds

P = 128
B, S, D = 4, 1024, 128
TOK = B * S
NT = TOK // P
CH = 512
NCH = TOK // CH
EPS = 1e-5
NEG = -1e30


class Count:

    def __init__(self, k, name, credit=0):
        self.sem = k.sem(name)
        self.base = credit
        self.credit = credit

    def seed(self, eng):
        eng.sem_inc(self.sem, self.credit)

    def at(self, n):
        return n + (self.base + 1)

    def advance(self, n):
        self.base += n


class Steps:

    def __init__(self, k, engine, items):
        self.sem, self.base = k.step_sems[engine], k.step_base[engine]
        self.pos, self.order, self.emitted = {}, [], []
        self.total = self._lay(items, 0, ())
        k.step_base[engine] += self.total

    @staticmethod
    def _size(items):
        return sum(1 if isinstance(x, str) else x[0] * Steps._size(x[1]) for x in items)

    def _lay(self, items, off, strides):
        for x in items:
            if isinstance(x, str):
                assert x not in self.pos, x
                self.pos[x] = (off, strides)
                self.order.append(x)
                off += 1
            else:
                one = self._size(x[1])
                self._lay(x[1], off, strides + (one,))
                off += x[0] * one
        return off

    def at(self, name, *rounds):
        off, strides = self.pos[name]
        assert len(rounds) == len(strides), name
        v = self.base + off + 1
        for r, s in zip(rounds, strides):
            v = r * s + v
        return v

    def done(self, ins, name):
        self.emitted.append(name)
        assert self.order[:len(self.emitted)] == self.emitted, (name, self.order[len(self.emitted) - 1])
        ins.then_inc(self.sem, 1)

    def close(self):
        assert self.emitted == self.order, self.order[len(self.emitted):]


class Kit:

    ENGINES = ("pe", "act", "dve", "pool")
    SEED = 64

    def __init__(self, nc, ctx, ins, out):
        self.nc, self.ctx, self.ins, self.out = nc, ctx, ins, out
        self.step_sems = {e: self.sem(f"{e}_steps") for e in self.ENGINES}
        self.step_base = {e: self.SEED for e in self.ENGINES}
        self.held = self.sem("held")

    def sem(self, name):
        return self.ctx.enter_context(self.nc.semaphore(name))

    def sb(self, name, shape, dt=F32, ctx=None):
        return (ctx or self.ctx).enter_context(self.nc.sbuf_tensor(name, shape, dt))


def when(eng, steps, name, *rounds):
    eng.wait_ge(steps.sem, steps.at(name, *rounds))


def hold(k, eng):
    eng.sem_inc(k.held, 1)


class Stream:

    def __init__(self, k, name, names, lead=2):
        self.names, self.lead = names, lead
        self.sem, self.next = k.sem(name), 0

    def seed(self, eng):
        eng.sem_inc(self.sem, self.lead * len(self.names))

    def at(self, name, n):
        return n * len(self.names) + (self.lead * len(self.names) + self.names.index(name) + 1)

    def done(self, ins, name):
        assert self.names[self.next] == name, (self.names[self.next], name)
        self.next = (self.next + 1) % len(self.names)
        ins.then_inc(self.sem, 1)


SMALL = 12


def load_stage(k):
    nc, ins = k.nc, k.ins
    k.x_tm = k.sb("x_tm", [P, NT, D])
    k.xnT = k.sb("xnT", [P, TOK])
    k.ident = k.sb("ident", [P, P])
    k.triu = k.sb("triu", [P, P])
    k.ones = k.sb("ones", [P, P])
    k.const = k.sb("const", [P, 4])
    k.ps = k.ctx.enter_context(nc.psum_tensor("ps", [P, 8, CH], F32))
    s_load = k.sem("s_load")
    steps = Steps(k, "pool", ["ones", "one", "eps", "halfpi", "zero"])
    with nc.Block() as block:
        @block.sync
        def _(sp):
            x = ins["x"].rearrange("b (j p) d -> p (b j) d", p=P)
            sp.dma_start(k.x_tm[:], x).then_inc(s_load, 16)
            sp.dma_start(k.ident[:], ins["ident"]).then_inc(s_load, 16)
            sp.dma_start(k.triu[:], ins["triu"]).then_inc(s_load, 16)
            sp.wait_ge(s_load, 48)

        @block.gpsimd
        def _(pool):
            pool.sem_inc(k.step_sems["pool"], Kit.SEED)
            steps.done(pool.memset(k.ones[:], 1.0), "ones")
            for i, (name, v) in enumerate((("one", 1.0), ("eps", EPS), ("halfpi", float(np.pi / 2)), ("zero", 0.0))):
                steps.done(pool.memset(k.const[:, i:i + 1], v), name)
            pool.wait_ge(steps.sem, steps.at("zero"))

        @block.vector
        def _(dve):
            dve.sem_inc(k.step_sems["dve"], Kit.SEED)

        @block.scalar
        def _(act):
            act.sem_inc(k.step_sems["act"], Kit.SEED)

        @block.tensor
        def _(pe):
            pe.sem_inc(k.step_sems["pe"], Kit.SEED)
    steps.close()
    k.one, k.eps, k.halfpi, k.zero = (k.const[:, i:i + 1] for i in range(4))


def norm_stage(k, tag, src, evacuate, keep=None):
    nc = k.nc
    with ExitStack() as ctx:
        stats = k.sb(f"{tag}_stats", [P, NT, 6], ctx=ctx)
        tmp = k.sb(f"{tag}_tmp", [P, 6, NT], ctx=ctx)
        xn = k.sb(f"{tag}_xn", [P, 2, 4, D], ctx=ctx)
        xm2 = k.sb(f"{tag}_mean_rstd", [P, 2, NT], ctx=ctx)
        mean, rstd = xm2[:, 0, :], xm2[:, 1, :]
        rounds = NCH // 2
        V = Steps(k, "dve", [(rounds, ["bn"]), "msum", "diff", "m2", "diff2", "var", "mean", "rstd",
                             (rounds, ["xn0", "xn1"])])
        A = Steps(k, "act", ["std", (rounds, ["xnT0", "xnT1"])])
        T = Steps(k, "pe", [(rounds, ["tr0", "tr1"])])
        G = Steps(k, "pool", [(rounds, ["keep0", "add0", "keep1", "add1"])] if keep is not None else [])
        with nc.Block() as block:
            @block.vector
            def _(dve):
                with dve.Fori(0, rounds) as i:
                    for u in range(8):
                        ins = dve.bn_stats(stats[:, i * 8 + u, :], src[:, i * 8 + u, :])
                    V.done(ins, "bn")
                when(dve, V, "bn", rounds - 1)
                me, ve, mo, vo = (stats[:, :, c] for c in (1, 2, 4, 5))
                V.done(dve.tensor_tensor(tmp[:, 0, :], me, mo, ALU.add), "msum")
                V.done(dve.tensor_tensor(tmp[:, 1, :], me, mo, ALU.subtract), "diff")
                V.done(dve.tensor_tensor(tmp[:, 2, :], ve, vo, ALU.add), "m2")
                when(dve, V, "m2")
                V.done(dve.scalar_tensor_tensor(out=tmp[:, 3, :], in0=tmp[:, 1, :], scalar=0.25,
                                                in1=tmp[:, 1, :], op0=ALU.mult, op1=ALU.mult), "diff2")
                when(dve, V, "diff2")
                V.done(dve.scalar_tensor_tensor(out=tmp[:, 4, :], in0=tmp[:, 2, :], scalar=1.0 / D,
                                                in1=tmp[:, 3, :], op0=ALU.mult, op1=ALU.add), "var")
                V.done(dve.tensor_scalar(mean, tmp[:, 0, :], 0.5, None, ALU.mult), "mean")
                when(dve, A, "std")
                V.done(dve.reciprocal(rstd, tmp[:, 5, :]), "rstd")
                when(dve, V, "rstd")
                with dve.Fori(0, rounds) as i:
                    for u in range(2):
                        when(dve, T, f"tr{u}", i - 1)
                        if keep is not None:
                            when(dve, G, f"add{u}", i - 1)
                        for t in range(4):
                            j = i * 8 + (u * 4 + t)
                            ins = dve.tensor_scalar(xn[:, u, t, :], src[:, j, :], mean[:, ds(j, 1)],
                                                    rstd[:, ds(j, 1)], ALU.subtract, ALU.mult)
                        V.done(ins, f"xn{u}")

            @block.scalar
            def _(act):
                when(act, V, "var")
                A.done(act.activation(tmp[:, 5, :], tmp[:, 4, :], ACT.Sqrt, bias=k.eps), "std")
                with act.Fori(0, rounds) as i:
                    for u in range(2):
                        when(act, T, f"tr{u}", i)
                        A.done(evacuate(act, i, u, k.ps[:, u, :]), f"xnT{u}")

            @block.tensor
            def _(pe):
                with pe.Fori(0, rounds) as i:
                    for u in range(2):
                        when(pe, V, f"xn{u}", i)
                        when(pe, A, f"xnT{u}", i - 1)
                        for t in range(4):
                            ins = pe.transpose(k.ps[:, u, t * P:(t + 1) * P], xn[:, u, t, :], k.ident[:])
                        T.done(ins, f"tr{u}")

            if keep is not None:
                @block.gpsimd
                def _(pool):
                    with pool.Fori(0, rounds) as i:
                        for u in range(2):
                            when(pool, V, f"xn{u}", i)
                            hold(k, pool)
                            tiles = ds(i * 8 + u * 4, 4)
                            G.done(pool.tensor_copy(keep[:, tiles, :], xn[:, u, :, :]), f"keep{u}")
                            G.done(pool.tensor_tensor(src[:, tiles, :], src[:, tiles, :], xn[:, u, :, :],
                                                      ALU.add), f"add{u}")
        for s in (V, A, T, G):
            s.close()


def to_xnT(k):
    return lambda act, i, u, bank: act.copy(k.xnT[:, ds((i * 2 + u) * CH, CH)], bank)


DI, NS, RANK, CONV = 2 * D, 16, D // 16, 4
HALF = DI // P
PAD = CONV - 1
ROW = S + 2 * PAD
NT_S = S // CH
UNROLL = 4


def selectors():
    r = np.arange(3 * 2 * NS)
    return (r[:, None] % (2 * NS) == np.arange(2 * NS)[None, :]).astype(np.float32)


def mamba_stage(k, d, pad, accF, ctx):
    nc, ins, back = k.nc, k.ins, d == "b"
    n = lambda x: f"m{d}_{x}"
    sb = lambda x, shape, dt=F32: k.sb(n(x), shape, dt, ctx=ctx)
    inw = sb("inw", [P, 2 * DI])
    cw = sb("convw", [P, CONV, DI])
    wk = sb("wk", [P, CONV, DI])
    xw = sb("xprojw", [P, HALF, 3 * 2 * NS + RANK])
    dtw = sb("dtw", [RANK, DI])
    col = sb("col", [P, 3, HALF])
    An = sb("A", [P, HALF, NS])
    outw = sb("outw", [P, HALF, D])
    pw = sb("projw", [P, D])
    u = sb("u", [P, HALF, S])
    zs = sb("zs", [P, HALF, S])
    delta = sb("delta", [P, HALF, S])
    du = sb("du", [P, HALF, S])
    soft = sb("soft", [P, HALF, S])
    tmp = soft[:, 0, :]
    dtlow = sb("dtlow", [RANK, S])
    split = sb("split", [96, S], BF16)
    part = sb("part", [96, S], BF16)
    rest = sb("rest", [96, S])
    row = sb("row", [96, 2 * NS])
    sel = sb("sel", [96, 2 * NS, P], BF16)
    b_sb = sb("b_sb", [P, UNROLL, CH])
    dBx = sb("dBx", [P, UNROLL, HALF, CH])
    h = sb("h", [P, 2, HALF, CH])
    hC = sb("hC", [P, 2, HALF, CH])
    carry = sb("carry", [P, NS, HALF])
    ps = k.ps
    bankB, bankC, bankA, bankY = 0, 2, 4, 6
    Z, DT = (6, 0), (2, 6)

    s_w = k.sem(n("weights"))
    b_ready, c_ready = Count(k, n("b_ready")), Count(k, n("c_ready"))
    b_copied = Count(k, n("b_copied"), credit=4)
    dA = Count(k, n("dA_ready"), credit=4)
    dBx_ready = Count(k, n("dBx_ready"), credit=HALF * UNROLL)
    scanned = Count(k, n("scanned"), credit=HALF * UNROLL)
    carried = Count(k, n("carried"))
    hC_ready = Count(k, n("hC_ready"), credit=4)
    summed = Count(k, n("summed"), credit=4)
    NU = NS * HALF

    T = Steps(k, "pe", [(B, ["xc0", "xc1", "z0", "xdb", "z1", "dt0", "dt1", "out0", "out1", "proj0", "proj1"])])
    A = Steps(k, "act", ["A", (B, ["u0", "u1", "z0", "hi", "dtlow", "part", "mid", "z1", "abs0", "abs1",
                                   "lo", "exp", "ln", "fo"])])
    V = Steps(k, "dve", ["sel", "wk", "A", (B, ["rest", "relu0", "rest2", "relu1", "delta0", "du0", "delta1", "du1", "delta2", "du2", "delta3", "du3", "y0", "y1", "y2", "y3", "acc"])])
    G = Steps(k, "pool", [(B, ["g0", "g1", "g2", "g3"])])

    def chunk(x):
        return NT_S - 1 - x if back else x

    def time(ap):
        return ap[:, ::-1] if back else ap

    with nc.Block() as block:
        @block.sync
        def _(sp):
            w = {q: ins[f"L0a_{d}_{q}"] for q in ("inWT", "convW", "xprojT", "dtWT", "A_log", "outWT",
                                                  "convb", "dtb", "Dskip")}
            halves = "(c p) n -> p c n"
            loads = [(inw[:], w["inWT"]),
                     (cw[:], w["convW"].partition_broadcast(P)),
                     *((xw[:, :, r * 32:r * 32 + 32], w["xprojT"][:, RANK:].rearrange(halves, p=P)) for r in range(3)),
                     (xw[:, :, 96:], w["xprojT"][:, :RANK].rearrange(halves, p=P)),
                     (dtw[:], w["dtWT"]),
                     (An[:], w["A_log"].rearrange(halves, p=P)),
                     (outw[:], w["outWT"].rearrange(halves, p=P)),
                     (pw[:], ins["L0a_projWT"][D * back:D * back + D, :]),
                     (row[:], ins["sel"])]
            loads += [(col[:, i, :], w[q].rearrange("(c p) -> p c", p=P)) for i, q in enumerate(("convb", "dtb", "Dskip"))]
            with nc.allow_non_contiguous_dma(reason="columns of small weights"):
                for dst, src in loads:
                    sp.dma_start(dst, src).then_inc(s_w, 16)
            sp.wait_ge(s_w, 16 * len(loads))
        n_w = 16 * 14

        @block.tensor
        def _(pe):
            summed.seed(pe)
            pe.wait_ge(s_w, n_w)
            when(pe, V, "wk")
            with pe.Fori(0, B) as b:
                when(pe, V, "acc", b - 1)

                def z(c, bank):
                    for t in range(NT_S):
                        mm = pe.matmul(ps[:, bank + t, :], inw[:, DI + c * P:DI + c * P + P],
                                       pad[:, ds(b * ROW + PAD + t * CH, CH)], start=True, stop=True)
                    T.done(mm, f"z{c}")

                for c in range(HALF):
                    for t in range(NT_S):
                        for tap in range(CONV):
                            shift = t * CH + (PAD + CONV - 1 - tap if back else tap)
                            mm = pe.matmul(ps[:, 2 * c + t, :], wk[:, tap, c * P:c * P + P],
                                           pad[:, ds(b * ROW + shift, CH)], start=tap == 0, stop=tap == CONV - 1)
                    T.done(mm, f"xc{c}")
                z(0, Z[0])
                when(pe, A, "u1", b)
                for t in range(NT_S):
                    for c in range(HALF):
                        mm = pe.matmul(ps[0:96 + RANK, 4 + t, :], xw[:, c, :], u[:, c, t * CH:t * CH + CH],
                                       start=c == 0, stop=c == HALF - 1)
                T.done(mm, "xdb")
                z(1, Z[1])
                when(pe, A, "dtlow", b)
                for c in range(HALF):
                    for t in range(NT_S):
                        mm = pe.matmul(ps[:, DT[c] + t, :], dtw[:, c * P:c * P + P], dtlow[:, t * CH:t * CH + CH],
                                       start=True, stop=True)
                    T.done(mm, f"dt{c}")
                when(pe, A, "lo", b)
                when(pe, V, "relu1", b)

                def rows(F):
                    t = chunk(F[0])
                    return split[:, t * CH:t * CH + CH]

                def broadcast_B(F, n):
                    pe.wait_ge(b_copied.sem, b_copied.at((b * NT_S + F[0]) * NS + F[1] - 2))
                    pe.matmul(ps[:, bankB + n, :], sel[:, F[1], :], rows(F), start=True, stop=True)\
                      .then_inc(b_ready.sem, 1)

                def broadcast_C(F, n):
                    pe.wait_ge(hC_ready.sem, hC_ready.at((b * NT_S + F[0]) * NU + (F[1] * HALF + HALF - 1 - 2 * HALF)))
                    pe.matmul(ps[:, bankC + n, :], sel[:, NS + F[1], :], rows(F), start=True, stop=True)\
                      .then_inc(c_ready.sem, 1)

                def add_up(F, n, first, last):
                    for c in range(HALF):
                        pe.wait_ge(hC_ready.sem, hC_ready.at((b * NT_S + F[0]) * NU + (F[1] * HALF + c)))
                        pe.matmul(ps[:, bankY + c, :], k.ident[:], hC[:, n, c, :], start=first, stop=last)\
                          .then_inc(summed.sem, 1)

                def state(x, s, j):
                    ahead = lambda m: (x, s + m) if not isinstance(s, int) or s + m < NS else (x + 1, s + m - NS)
                    if ahead(4)[0] < NT_S:
                        broadcast_B(ahead(4), j % 2)
                    first = isinstance(s, int) and s == 0
                    if first and x:
                        when(pe, V, f"y{HALF * x - 1}", b)
                    add_up((x, s), j % 2, first, isinstance(s, int) and s == NS - 1)
                    if ahead(2)[0] < NT_S:
                        broadcast_C(ahead(2), j % 2)

                for s in range(2):
                    broadcast_B((0, s), s)
                    broadcast_C((0, s), s)
                for s in range(2, 4):
                    broadcast_B((0, s), s % 2)
                for x in range(NT_S):
                    for s in range(UNROLL):
                        state(x, s, s)
                    with pe.Fori(1, NS // UNROLL - 1) as i:
                        for j in range(UNROLL):
                            state(x, i * UNROLL + j, j)
                    for s in range(NS - UNROLL, NS):
                        state(x, s, s)
                when(pe, G, "g3", b)
                for t in range(NT_S):
                    for c in range(HALF):
                        mm = pe.matmul(ps[:, t, :], outw[:, c, :], zs[:, c, t * CH:t * CH + CH],
                                       start=c == 0, stop=c == HALF - 1)
                    T.done(mm, f"out{t}")
                when(pe, A, "fo", b)
                for t in range(NT_S):
                    T.done(pe.matmul(ps[:, 2 + t, :], pw[:], tmp[:, t * CH:t * CH + CH], start=True, stop=True),
                           f"proj{t}")

        @block.scalar
        def _(act):
            for cnt in (b_copied, dA):
                cnt.seed(act)
            act.wait_ge(s_w, n_w)
            A.done(act.activation(An[:], An[:], ACT.Exp), "A")
            when(act, V, "A")
            with act.Fori(0, B) as b:
                when(act, G, "g3", b - 1)
                when(act, V, "acc", b - 1)
                when(act, T, "proj1", b - 1)

                def z(c):
                    when(act, T, f"z{c}", b)
                    A.done(act.activation(zs[:, c, :], ps[:, Z[c]:Z[c] + 2, :].rearrange("p a n -> p (a n)"),
                                          ACT.Silu), f"z{c}")

                for c in range(HALF):
                    when(act, T, f"xc{c}", b)
                    A.done(act.activation(u[:, c, :], ps[:, 2 * c:2 * c + 2, :].rearrange("p a n -> p (a n)"),
                                          ACT.Silu, bias=col[:, 0, c:c + 1]), f"u{c}")
                z(0)
                when(act, T, "xdb", b)
                A.done(act.copy(split[:], ps[0:96, 4:6, :].rearrange("p a n -> p (a n)")), "hi")
                A.done(act.copy(dtlow[:], ps[96:96 + RANK, 4:6, :].rearrange("p a n -> p (a n)")), "dtlow")
                when(act, V, "rest", b)
                A.done(act.copy(part[64:96, :], rest[64:96, :]), "part")
                A.done(act.copy(split[32:64, :], rest[32:64, :]), "mid")
                z(1)
                for c in range(HALF):
                    when(act, V, f"relu{c}", b)
                    A.done(act.activation(soft[:, c, :], ps[:, DT[c]:DT[c] + 2, :].rearrange("p a n -> p (a n)"),
                                          ACT.Abs, bias=col[:, 1, c:c + 1]), f"abs{c}")
                when(act, V, "rest2", b)
                A.done(act.copy(split[64:96, :], rest[64:96, :]), "lo")
                when(act, A, "abs1", b)
                A.done(act.activation(soft[:], soft[:], ACT.Exp, scale=-1.0), "exp")
                when(act, A, "exp", b)
                A.done(act.activation(soft[:], soft[:], ACT.Ln, bias=k.one), "ln")

                def copy_B(F, j):
                    act.wait_ge(b_ready.sem, b_ready.at((b * NT_S + F[0]) * NS + F[1]))
                    act.wait_ge(dBx_ready.sem,
                                dBx_ready.at((b * NT_S + F[0]) * NU + (F[1] * HALF + HALF - 1 - HALF * UNROLL)))
                    return act.copy(b_sb[:, j % UNROLL, :], ps[:, bankB + j % 2, :])

                def decay(F, j):
                    t = chunk(F[0])
                    for c in range(HALF):
                        act.wait_ge(scanned.sem, scanned.at((b * NT_S + F[0]) * NU + (F[1] * HALF + c - HALF)))
                        act.activation(ps[:, bankA + c, :], delta[:, c, t * CH:t * CH + CH], ACT.Exp,
                                       scale=An[:, c, ds(F[1], 1)]).then_inc(dA.sem, 1)

                for s in range(2):
                    copy_B((0, s), s).then_inc(b_copied.sem, 1)
                for x in range(NT_S):
                    when(act, V, f"delta{x * HALF + 1}", b)
                    hold(k, act)
                    with act.Fori(0, NS // UNROLL - 1) as i:
                        for j in range(UNROLL):
                            copy_B((x, i * UNROLL + (j + 2)), j + 2).then_inc(b_copied.sem, 1)
                            decay((x, i * UNROLL + j), j)
                    for s in range(NS - UNROLL, NS):
                        if s + 2 < NS:
                            copy_B((x, s + 2), s + 2).then_inc(b_copied.sem, 1)
                        elif x + 1 < NT_S:
                            copy_B((x + 1, s + 2 - NS), s + 2).then_inc(b_copied.sem, 1)
                        decay((x, s), s)
                when(act, T, "out1", b)
                A.done(act.copy(tmp[:], ps[:, 0:2, :].rearrange("p a n -> p (a n)")), "fo")

        @block.gpsimd
        def _(pool):
            dBx_ready.seed(pool)
            with pool.Fori(0, B) as b:
                for x in range(NT_S):
                    when(pool, V, f"du{x * HALF + 1}", b)
                    hold(k, pool)
                    t = chunk(x)
                    with pool.Fori(0, NS // UNROLL) as i:
                        for j in range(UNROLL):
                            s, su = (b * NT_S + x) * NS + (i * UNROLL + j), (b * NT_S + x) * NU + (i * UNROLL + j) * HALF
                            pool.wait_ge(b_copied.sem, b_copied.at(s))
                            for c in range(HALF):
                                pool.wait_ge(scanned.sem, scanned.at(su + c - UNROLL * HALF))
                                pool.tensor_tensor(dBx[:, j, c, :], du[:, c, t * CH:t * CH + CH],
                                                   b_sb[:, j, :], ALU.mult).then_inc(dBx_ready.sem, 1)
                    for c in range(HALF):
                        when(pool, V, f"y{HALF * x + c}", b)
                        g = zs[:, c, t * CH:t * CH + CH]
                        G.done(pool.tensor_tensor(g, g, u[:, c, t * CH:t * CH + CH], ALU.mult), f"g{HALF * x + c}")

        @block.vector
        def _(dve):
            for cnt in (scanned, hC_ready):
                cnt.seed(dve)
            dve.wait_ge(s_w, n_w)
            V.done(dve.tensor_copy(sel[:], row[:].unsqueeze(2).to_broadcast([96, 2 * NS, P])), "sel")
            V.done(dve.tensor_tensor(wk[:], cw[:], inw[:, 0:DI].unsqueeze(1).to_broadcast([P, CONV, DI]), ALU.mult), "wk")
            when(dve, A, "A")
            V.done(dve.tensor_scalar(An[:], An[:], -1.0, None, ALU.mult), "A")
            with dve.Fori(0, B) as b:
                when(dve, A, "dtlow", b)
                V.done(dve.tensor_tensor(rest[:], ps[0:96, 4:6, :].rearrange("p a n -> p (a n)"), split[:],
                                         ALU.subtract), "rest")
                for c in range(HALF):
                    if c == 1:
                        when(dve, A, "part", b)
                        V.done(dve.tensor_tensor(rest[64:96, :], rest[64:96, :], part[64:96, :], ALU.subtract), "rest2")
                    when(dve, T, f"dt{c}", b)
                    V.done(dve.tensor_scalar(delta[:, c, :], ps[:, DT[c]:DT[c] + 2, :].rearrange("p a n -> p (a n)"),
                                             col[:, 1, c:c + 1], 0.0, ALU.add, ALU.max), f"relu{c}")
                when(dve, A, "ln", b)
                when(dve, V, "relu1", b)
                for x in range(NT_S):
                    for c in range(HALF):
                        cols = slice(chunk(x) * CH, chunk(x) * CH + CH)
                        V.done(dve.tensor_tensor(delta[:, c, cols], delta[:, c, cols], soft[:, c, cols], ALU.add),
                               f"delta{x * HALF + c}")
                        when(dve, V, f"delta{x * HALF + c}", b)
                        V.done(dve.tensor_tensor(du[:, c, cols], delta[:, c, cols], u[:, c, cols], ALU.mult),
                               f"du{x * HALF + c}")
                for x in range(NT_S):
                    t = chunk(x)
                    with dve.Fori(0, NS // UNROLL) as i:
                        for j in range(UNROLL):
                            n_s = i * UNROLL + j
                            s, su = (b * NT_S + x) * NS + n_s, (b * NT_S + x) * NU + n_s * HALF
                            for c in range(HALF):
                                dve.wait_ge(dA.sem, dA.at(su + c))
                                dve.wait_ge(dBx_ready.sem, dBx_ready.at(su + c))
                                dve.wait_ge(hC_ready.sem, hC_ready.at(su + c - 2 * HALF))
                                first = 0.0 if x == 0 else carry[:, n_s, c:c + 1]
                                dve.tensor_tensor_scan(time(h[:, j % 2, c, :]), time(ps[:, bankA + c, :]),
                                                       time(dBx[:, j, c, :]), first, ALU.mult, ALU.add)\
                                   .then_inc(scanned.sem, 1)
                            dve.wait_ge(c_ready.sem, c_ready.at(s))
                            for c in range(HALF):
                                dve.wait_ge(scanned.sem, scanned.at(su + c))
                                dve.wait_ge(summed.sem, summed.at(su + c - 2 * HALF))
                                dve.tensor_tensor(hC[:, j % 2, c, :], h[:, j % 2, c, :], ps[:, bankC + j % 2, :],
                                                  ALU.mult).then_inc(hC_ready.sem, 1)
                            if x == 0:
                                dve.wait_ge(scanned.sem, scanned.at(su + (HALF - 1)))
                                end = 0 if back else CH - 1
                                dve.tensor_copy(carry[:, n_s, :], h[:, j % 2, :, end]).then_inc(carried.sem, 1)
                    if x == 0:
                        dve.wait_ge(carried.sem, carried.at(b * NS + (NS - 1)))
                    for c in range(HALF):
                        dve.wait_ge(summed.sem, summed.at((b * NT_S + x) * NU + (NU - HALF + c)))
                        uc = u[:, c, t * CH:t * CH + CH]
                        V.done(dve.scalar_tensor_tensor(out=uc, in0=uc, scalar=col[:, 2, c:c + 1],
                                                        in1=ps[:, bankY + c, :], op0=ALU.mult, op1=ALU.add),
                               f"y{HALF * x + c}")
                when(dve, T, "proj1", b)
                acc = accF[:, ds(b * S, S)]
                src = ps[:, 2:4, :].rearrange("p a n -> p (a n)")
                if back:
                    V.done(dve.tensor_tensor(acc, acc, src, ALU.add), "acc")
                else:
                    V.done(dve.tensor_copy(acc, src), "acc")
    for s in (T, A, V, G):
        s.close()


NE = 8


def top2_names(tag):
    return [f"{tag}_{x}" for x in ("m1", "eq1", "w1", "i1", "hot1", "less", "m2", "eq2", "w2", "i2", "hot2")]


def top2(dve, V, tag, v, work, hot, m, iota):
    wide = lambda x: x.unsqueeze(2).to_broadcast([P, NT, NE])
    iotas = iota.unsqueeze(1).to_broadcast([P, NT, NE])
    steps = iter(top2_names(tag))

    def step(ins):
        name = next(steps)
        V.done(ins, name)
        when(dve, V, name)

    for r in range(2):
        step(dve.tensor_reduce(m[:, r, :], v, AX_X, ALU.max))
        step(dve.tensor_tensor(work[:, 0], v, wide(m[:, r, :]), ALU.is_equal))
        step(dve.tensor_tensor(work[:, 0], work[:, 0], iotas, ALU.mult))
        step(dve.tensor_reduce(m[:, 2, :], work[:, 0], AX_X, ALU.min))
        step(dve.tensor_tensor(hot[:, r], iotas, wide(m[:, 2, :]), ALU.is_equal))
        if r == 0:
            step(dve.scalar_tensor_tensor(out=work[:, 1], in0=hot[:, 0], scalar=-3e38, in1=v,
                                          op0=ALU.mult, op1=ALU.add))
            v = work[:, 1]


def moe0_stage(k, accF):
    nc, ins = k.nc, k.ins
    with ExitStack() as ctx:
        sb = lambda x, shape, dt=F32: k.sb("e0_" + x, shape, dt, ctx=ctx)
        gw, gb = sb("gate_w", [P, NE]), sb("gate_b", [P, NE])
        iota = sb("iota", [P, NE])
        ew, eb = sb("expert_w", [P, NE, D]), sb("expert_b", [P, NE])
        gate, work, hot = sb("gate", [P, NT, NE]), sb("work", [P, 2, NT, NE]), sb("hot", [P, 2, NT, NE])
        m = sb("m", [P, 3, NT])
        cnt, scale, bias = sb("cnt", [P, NE]), sb("scale", [P, NE]), sb("bias", [P, NE])
        r = sb("r", [P, 2, CH])
        s_w = k.sem("s_e0_weights")
        T = Steps(k, "pe", ["gate", "counts"])
        V = Steps(k, "dve", ["gate"] + top2_names("g") + ["both", "cnt", "scale", "bias"])
        expert = Count(k, "e0_expert", credit=4)
        relu = Count(k, "e0_relu", credit=4)
        added = Count(k, "e0_added", credit=4)
        with nc.Block() as block:
            @block.sync
            def _(sp):
                for dst, src in ((gw[:], ins["L0f_gateT"]), (gb[:], ins["L0f_gate_b"].partition_broadcast(P)),
                                 (iota[:], ins["iota"].partition_broadcast(P)), (ew[:], ins["L0f_expertT"]),
                                 (eb[:], ins["L0f_expert_bT"])):
                    sp.dma_start(dst, src).then_inc(s_w, 16)
                sp.wait_ge(s_w, 5 * 16)

            @block.tensor
            def _(pe):
                expert.seed(pe)
                pe.wait_ge(s_w, 5 * 16)
                for j in range(NT):
                    mm = pe.matmul(k.ps[:, 7, j * NE:j * NE + NE], k.xnT[:, j * P:j * P + P], gw[:],
                                   start=True, stop=True)
                T.done(mm, "gate")
                when(pe, V, "cnt")
                T.done(pe.matmul(k.ps[:, 6, 0:NE], k.ones[:], cnt[:], start=True, stop=True), "counts")
                with pe.Fori(0, NCH) as i:
                    for e in range(NE):
                        pe.wait_ge(relu.sem, relu.at(i * NE + (e - 4)))
                        pe.matmul(k.ps[:, e % 4, :], ew[:, e, :], k.xnT[:, ds(i * CH, CH)], start=True,
                                  stop=True).then_inc(expert.sem, 1)

            @block.vector
            def _(dve):
                added.seed(dve)
                when(dve, T, "gate")
                V.done(dve.tensor_tensor(gate[:], k.ps[:, 7, 0:NT * NE].rearrange("p (t e) -> p t e", e=NE),
                                         gb[:].unsqueeze(1).to_broadcast([P, NT, NE]), ALU.add), "gate")
                when(dve, V, "gate")
                top2(dve, V, "g", gate[:], work, hot, m, iota[:])
                V.done(dve.tensor_tensor(work[:, 0], hot[:, 0], hot[:, 1], ALU.add), "both")
                when(dve, V, "both")
                V.done(dve.tensor_reduce(cnt[:], work[:, 0].rearrange("p t e -> p e t"), AX_X, ALU.add), "cnt")
                when(dve, T, "counts")
                V.done(dve.tensor_scalar(scale[:], k.ps[:, 6, 0:NE], 1.0 / (2 * TOK), None, ALU.mult), "scale")
                when(dve, V, "scale")
                V.done(dve.tensor_tensor(bias[:], eb[:], scale[:], ALU.mult), "bias")
                with dve.Fori(0, NCH) as i:
                    for e in range(NE):
                        dve.wait_ge(relu.sem, relu.at(i * NE + e))
                        dve.wait_ge(added.sem, added.at(i * NE + (e - 1)))
                        acc = accF[:, ds(i * CH, CH)]
                        dve.tensor_tensor(acc, acc, r[:, e % 2, :], ALU.add).then_inc(added.sem, 1)

            @block.scalar
            def _(act):
                relu.seed(act)
                when(act, V, "bias")
                with act.Fori(0, NCH) as i:
                    for e in range(NE):
                        act.wait_ge(expert.sem, expert.at(i * NE + e))
                        act.wait_ge(added.sem, added.at(i * NE + (e - 2)))
                        act.activation(r[:, e % 2, :], k.ps[:, e % 4, :], ACT.Relu, scale=scale[:, e:e + 1],
                                       bias=bias[:, e:e + 1]).then_inc(relu.sem, 1)
        T.close()
        V.close()


def add_back_stage(k, tag, accF, bias=None):
    nc = k.nc
    rounds = NCH // 2
    with ExitStack() as ctx:
        slot = k.sb(f"{tag}_slot", [P, 2, CH], ctx=ctx)
        col = k.sb(f"{tag}_bias", [P, 1], ctx=ctx)
        s_b = k.sem(f"s_{tag}_bias")
        A = Steps(k, "act", [(rounds, ["slot0", "slot1"])])
        T = Steps(k, "pe", [(rounds, ["tr0", "tr1"])])
        V = Steps(k, "dve", [(rounds, ["add0", "add1"])])
        with nc.Block() as block:
            if bias is not None:
                @block.sync
                def _(sp):
                    sp.dma_start(col[:], bias.rearrange("(p a) -> p a", a=1)).then_inc(s_b, 16)
                    sp.wait_ge(s_b, 16)

            @block.scalar
            def _(act):
                if bias is not None:
                    act.wait_ge(s_b, 16)
                with act.Fori(0, rounds) as i:
                    for u in range(2):
                        when(act, T, f"tr{u}", i - 1)
                        src = accF[:, ds((i * 2 + u) * CH, CH)]
                        A.done(act.copy(slot[:, u, :], src) if bias is None else
                               act.activation(slot[:, u, :], src, ACT.Identity, bias=col[:]), f"slot{u}")

            @block.tensor
            def _(pe):
                with pe.Fori(0, rounds) as i:
                    for u in range(2):
                        when(pe, A, f"slot{u}", i)
                        when(pe, V, f"add{u}", i - 1)
                        for t in range(4):
                            mm = pe.transpose(k.ps[:, u, t * P:t * P + P], slot[:, u, t * P:t * P + P], k.ident[:])
                        T.done(mm, f"tr{u}")

            @block.vector
            def _(dve):
                with dve.Fori(0, rounds) as i:
                    for u in range(2):
                        when(dve, T, f"tr{u}", i)
                        x = k.x_tm[:, ds(i * 8 + u * 4, 4), :]
                        V.done(dve.tensor_tensor(x, x, k.ps[:, u, :].rearrange("p (t d) -> p t d", d=D), ALU.add),
                               f"add{u}")
        for s in (A, T, V):
            s.close()


HEADS, HD = 16, D // 16


def attn1_stage(k, accF):
    nc, ins = k.nc, k.ins
    with ExitStack() as ctx:
        sb = lambda x, shape, dt=F32: k.sb("b1_" + x, shape, dt, ctx=ctx)
        w, sg = sb("w", [P, 4]), sb("signs", [P, 4])
        qk, head = sb("qk", [P, 1]), sb("head", [P, P])
        prod = sb("prod", [P, B, B, CH])
        att = sb("att", [P, 2, CH])
        o = sb("o", [P, B, CH])
        s_w = k.sem("s_b1_weights")
        HALVES = S // CH
        pairs = [(n, m) for n in range(B) for m in range(B)]
        V = Steps(k, "dve", ["diff", "ste", "qk", "head", (HALVES, [f"p{n}{m}" for n, m in pairs if n <= m]
                             + [x for n, m in pairs for x in (f"a{n}{m}", f"o{n}{m}")])])
        G = Steps(k, "pool", [(HALVES, [f"{x}{n}" for n in range(B) for x in ("f", "g", "h")])])
        T = Steps(k, "pe", [(HALVES, [f"s{n}{m}" for n, m in pairs])])
        A = Steps(k, "act", ["sign", (HALVES, [f"sign{n}" for n in range(B)])])
        with nc.Block() as block:
            @block.sync
            def _(sp):
                with nc.allow_non_contiguous_dma(reason="four columns"):
                    sp.dma_start(w[:], ins["L1a_w"].rearrange("r p -> p r")).then_inc(s_w, 16)
                sp.dma_start(head[:], ins["head_blocks"]).then_inc(s_w, 16)
                sp.wait_ge(s_w, 32)

            @block.vector
            def _(dve):
                when(dve, A, "sign")
                V.done(dve.tensor_tensor(sg[:], sg[:], w[:], ALU.subtract), "diff")
                when(dve, V, "diff")
                V.done(dve.tensor_tensor(sg[:], sg[:], w[:], ALU.add), "ste")
                when(dve, V, "ste")
                V.done(dve.scalar_tensor_tensor(out=qk[:], in0=sg[:, 0:1], scalar=float(HD) ** -0.5, in1=sg[:, 1:2],
                                                op0=ALU.mult, op1=ALU.mult), "qk")
                when(dve, V, "qk")
                V.done(dve.tensor_scalar(head[:], head[:], qk[:], None, ALU.mult), "head")
                with dve.Fori(0, HALVES) as i:
                    x = [k.xnT[:, ds(i * CH + n * S, CH)] for n in range(B)]
                    when(dve, T, f"s{B - 1}{B - 1}", i - 1)
                    for n, m in pairs:
                        if n <= m:
                            V.done(dve.tensor_tensor(prod[:, n, m, :], x[n], x[m], ALU.mult), f"p{n}{m}")
                    for q, (n, m) in enumerate(pairs):
                        when(dve, T, f"s{n}{m}", i)
                        if q >= 1:
                            pn, pm = pairs[q - 1]
                            when(dve, V, f"o{pn}{pm}", i)
                        V.done(dve.scalar_tensor_tensor(out=att[:, q % 2, :], in0=k.ps[:, q % 8, :], scalar=0.0,
                                                        in1=x[m], op0=ALU.is_gt, op1=ALU.mult), f"a{n}{m}")
                        when(dve, V, f"a{n}{m}", i)
                        if m == 0:
                            when(dve, G, f"h{n}", i - 1)
                        V.done(dve.tensor_scalar(o[:, n, :], att[:, q % 2, :], sg[:, 2:3], None, ALU.mult) if m == 0 else
                               dve.scalar_tensor_tensor(out=o[:, n, :], in0=att[:, q % 2, :], scalar=sg[:, 2:3],
                                                        in1=o[:, n, :], op0=ALU.mult, op1=ALU.add), f"o{n}{m}")

            @block.tensor
            def _(pe):
                pe.wait_ge(s_w, 32)
                when(pe, V, "head")
                with pe.Fori(0, HALVES) as i:
                    for q, (n, m) in enumerate(pairs):
                        when(pe, V, f"p{min(n, m)}{max(n, m)}", i)
                        if q < 8:
                            when(pe, V, "a%d%d" % pairs[q + 8], i - 1)
                        else:
                            when(pe, V, "a%d%d" % pairs[q - 8], i)
                        T.done(pe.matmul(k.ps[:, q % 8, :], head[:], prod[:, min(n, m), max(n, m), :], start=True,
                                         stop=True), f"s{n}{m}")

            @block.scalar
            def _(act):
                act.wait_ge(s_w, 32)
                A.done(act.activation(sg[:], w[:], ACT.Sign), "sign")
                with act.Fori(0, HALVES) as i:
                    for n in range(B):
                        when(act, V, f"o{n}{B - 1}", i)
                        A.done(act.activation(accF[:, ds(i * CH + n * S, CH)], o[:, n, :], ACT.Sign), f"sign{n}")

            @block.gpsimd
            def _(pool):
                with pool.Fori(0, HALVES) as i:
                    for n in range(B):
                        acc = accF[:, ds(i * CH + n * S, CH)]
                        when(pool, A, f"sign{n}", i)
                        hold(k, pool)
                        G.done(pool.tensor_tensor(acc, acc, o[:, n, :], ALU.subtract), f"f{n}")
                        when(pool, G, f"f{n}", i)
                        hold(k, pool)
                        G.done(pool.tensor_tensor(acc, acc, o[:, n, :], ALU.add), f"g{n}")
                        when(pool, G, f"g{n}", i)
                        hold(k, pool)
                        G.done(pool.tensor_tensor(acc, acc, sg[:, 3:4].to_broadcast([P, CH]), ALU.mult), f"h{n}")
        for s in (V, G, T, A):
            s.close()


DFF = 4 * D
FT = DFF // P


def experts1_stage(k, accF):
    nc, ins = k.nc, k.ins
    rounds = NE // 2
    with ExitStack() as ctx:
        sb = lambda x, shape, dt=F32: k.sb("e1_" + x, shape, dt, ctx=ctx)
        w1 = sb("w1", [P, 2, DFF])
        w2 = sb("w2", [P, 2, FT, D])
        b1 = sb("b1", [P, NE, FT])
        b2 = sb("b2", [P, NE, D])
        xs = sb("x", [P, 2, CH])
        h = sb("h", [P, 2, FT, CH])
        att = sb("att", [P, 2, CH])
        s_b = k.sem("s_e1_biases")
        s_w = [k.sem(f"s_e1_weights{u}") for u in range(2)]
        T = Steps(k, "pe", [(rounds, [f"{x}{u}" for u in range(2) for x in ("h0", "h1", "h2", "h3", "y")])])
        A = Steps(k, "act", [(rounds, [f"{x}{u}" for u in range(2) for x in ("att", "h0", "h1", "h2", "h3")])])
        V = Steps(k, "dve", [(rounds, [f"{x}{u}" for u in range(2) for x in ("bias", "add")])])
        with nc.Block() as block:
            @block.sync
            def _(sp):
                sp.dma_start(b1[:], ins["L1f_b1T"]).then_inc(s_b, 16)
                sp.dma_start(b2[:], ins["L1f_b2"].partition_broadcast(P)).then_inc(s_b, 16)
                with sp.Fori(0, rounds) as i:
                    for u in range(2):
                        when(sp, T, f"y{u}", i - 1)
                        sp.dma_start(w1[:, u, :], ins["L1f_w1T"][:, ds(i * 2 + u, 1), :].rearrange("p a n -> p (a n)"))\
                          .then_inc(s_w[u], 16)
                        sp.dma_start(w2[:, u, :, :], ins["L1f_w2T"][:, ds(i * 2 + u, 1), :, :]
                                     .rearrange("p a t n -> p (a t) n")).then_inc(s_w[u], 16)
                sp.wait_ge(s_b, 32)
                for u in range(2):
                    sp.wait_ge(s_w[u], 32 * rounds)

            @block.tensor
            def _(pe):
                with pe.Fori(0, rounds) as i:
                    for u in range(2):
                        pe.wait_ge(s_w[u], (i + 1) * 32)
                        x = k.xnT[:].rearrange("p (b e c) -> p b (e c)", b=B, c=P)[:, :, ds((i * 2 + u) * P, P)]
                        for f in range(FT):
                            if u == 0:
                                when(pe, A, f"h{f}1", i - 1)
                            else:
                                when(pe, A, f"h{f}0", i)
                            T.done(pe.matmul(k.ps[:, f, :], w1[:, u, f * P:f * P + P], x, start=True, stop=True),
                                   f"h{f}{u}")
                        when(pe, V, f"add{u}", i - 1)
                        for b in range(B):
                            y = k.ps[:, 4 + u, b * P:b * P + P]
                            when(pe, A, f"att{u}", i)
                            pe.matmul(y, att[:, u, b * P:b * P + P], k.ident[:], start=b == 0, stop=False,
                                      skip_group_check=True)
                            for f in range(FT):
                                if b == 0:
                                    when(pe, A, f"h{f}{u}", i)
                                mm = pe.matmul(y, h[:, u, f, b * P:b * P + P], w2[:, u, f, :], start=False,
                                               stop=b == B - 1 and f == FT - 1, skip_group_check=True)
                        T.done(mm, f"y{u}")

            @block.scalar
            def _(act):
                act.wait_ge(s_b, 32)
                with act.Fori(0, rounds) as i:
                    for u in range(2):
                        when(act, T, f"y{u}", i - 1)
                        src = accF[:].rearrange("p (b e c) -> p b (e c)", b=B, c=P)[:, :, ds((i * 2 + u) * P, P)]
                        A.done(act.copy(att[:, u, :].rearrange("p (b c) -> p b c", b=B), src), f"att{u}")
                        for f in range(FT):
                            when(act, T, f"h{f}{u}", i)
                            A.done(act.activation(h[:, u, f, :], k.ps[:, f, :], ACT.Gelu,
                                                  bias=b1[:, ds(i * 2 + u, 1), f]), f"h{f}{u}")

            @block.vector
            def _(dve):
                dve.wait_ge(s_b, 32)
                with dve.Fori(0, rounds) as i:
                    for u in range(2):
                        x = k.x_tm[:].rearrange("p (b e) d -> p b e d", b=B)[:, :, ds(i * 2 + u, 1), :]
                        bias = b2[:, ds(i * 2 + u, 1), :].to_broadcast([P, B, D])
                        x = x.rearrange("p b a d -> p b (a d)")
                        V.done(dve.tensor_tensor(x, x, bias, ALU.add), f"bias{u}")
                        when(dve, V, f"bias{u}", i)
                        when(dve, T, f"y{u}", i)
                        V.done(dve.tensor_tensor(x, x, k.ps[:, 4 + u, :].rearrange("p (b d) -> p b d", d=D), ALU.add),
                               f"add{u}")
        for s in (T, A, V):
            s.close()


H2, HP = 4, 64
DI2 = H2 * HP
NANG = 32
Z0, X0, B0, SM0 = 0, DI2, 2 * DI2, 2 * DI2 + 2 * P
NSM = 3 * H2 + NANG
CPB = S // P
TURN = (6.28125, float(np.float32(round((2 * np.pi - 6.28125) * 2 ** 21) / 2 ** 21)),)
TURN += (float(2 * np.pi - TURN[0] - TURN[1]),)
ROUND = 1.5 * 2.0 ** 23


def flat(ap):
    return ap.rearrange("p a n -> p (a n)") if len(ap.shape) == 3 else ap.rearrange("p a b n -> p (a b n)")


def mamba3_gates_stage(k, L):
    nc, ins = k.nc, k.ins
    with ExitStack() as ctx:
        sb = lambda x, shape, dt=F32: k.sb("g2_" + x, shape, dt, ctx=ctx)
        sm, pre = sb("small", [P, NT, NSM]), sb("pre", [P, 2, NT, H2])
        t1, t2, t3 = (sb(f"t{i}", [P, 2, NT, H2]) for i in range(3))
        lam, q, w1 = sb("lam", [P, NT, H2]), sb("q", [P, NT + 1, H2]), sb("w1", [P, NT, H2])
        ang, turn = sb("ang", [P, NT, H2 * NANG]), L["cos"]
        run = sb("run", [P, B, H2 * NANG])
        xs, squares = L["sin"], L["cos"]
        ssq = sb("ssq", [P, NT, 2])
        rounds = NT // 8
        shift, corner = sb("shift", [P, P]), sb("corner", [P, P])
        dtb, keep, nw = sb("dt_bias", [P, H2]), sb("keep", [P, NT, H2]), sb("norm_w", [P, 2, P])
        wt, neg, alpha, wsum = sb("ternary", [P, P]), sb("neg", [P, P]), sb("alpha", [P, 1]), sb("wsum", [P, 2])
        dpar = sb("D", [P, H2])
        s_w = k.sem("s_g2_weights")
        winT = L["winT"]
        A = Steps(k, "act", ["wabs", (NCH, ["z0", "z1"]), (rounds, ["xs0", "xs1", "sq0", "sq1"]),
                             "sm", "rms", "exp", "ln", "etrap", "eend", "ewb", (CPB, ["th"]), "sin", "abs", "cos"])
        T = Steps(k, "pe", ["wsum", (NCH, ["z0", "z1"]), (rounds, ["x0", "x1"]), "sm", "cum", "end", "shift", (CPB, ["th"])])
        V = Steps(k, "dve", ["delta", "pos", "neg", "tern", "weff", "dI", (rounds, ["bc0", "bc1", "ss0", "ss1"]),
                             "rstd", "pre", "preA", "relu", "nabs", "sp", "u1", "u1b", "corr",
                             "afloor", "adt", "lam", "lamr", "wdiag", "qlam", "q", "v", "w1", "cum", "wb", "wbe", "wbk",
                             "ang", "bcn", "bcw", "k1", "k2", "r1", "r2", "r3", "clamp"])
        G = Steps(k, "pool", ["qz", "run0", (CPB, ["run"]), "cend"])
        with nc.Block() as block:
            @block.sync
            def _(sp):
                loads = [(winT[:], ins["L2a_winT"]), (wt[:], ins["L2f_weightT"]),
                         (L["woutT"][:], ins["L2a_woutT"].rearrange("(c p) n -> p c n", p=P)),
                         (shift[:], ins["shift"]), (corner[:], ins["corner"]),
                         (L["maskneg"][:], ins["maskneg"]), (L["strict"][:], ins["strict"]),
                         (dtb[:], ins["L2a_dt_bias"].partition_broadcast(P)),
                         (dpar[:], ins["L2a_D_param"].partition_broadcast(P)),
                         (nw[:], ins["L2a_norm_w"].partition_broadcast(P)),
                         (L["hbias"][:], ins["L2a_head_bias"].partition_broadcast(P)),
                         (keep[:], ins["keep"].partition_broadcast(P)),
                         (alpha[:], ins["L2f_alpha"].partition_broadcast(P)),
                         (L["bias"][:], ins["L2f_bias"].rearrange("(a n) -> a n", a=1))]
                for dst, src in loads:
                    sp.dma_start(dst, src).then_inc(s_w, 16)
                sp.wait_ge(s_w, 16 * len(loads))
            n_w = 16 * 14

            @block.tensor
            def _(pe):
                pe.wait_ge(s_w, n_w)
                when(pe, A, "wabs")
                T.done(pe.matmul(k.ps[:, 7, 0:1], k.ones[:], wsum[:, 0:1], start=True, stop=True), "wsum")
                with pe.Fori(0, NCH) as i:
                    for c in range(2):
                        when(pe, A, f"z{c}", i - 1)
                        T.done(pe.matmul(k.ps[:, c, :], winT[:, Z0 + c * P:Z0 + c * P + P], k.xnT[:, ds(i * CH, CH)],
                                         start=True, stop=True), f"z{c}")
                with pe.Fori(0, rounds) as i:
                    for u in range(2):
                        when(pe, A, f"xs{u}", i)
                        when(pe, V, f"bc{u}", i - 1)
                        for t in range(4):
                            mm = pe.matmul(k.ps[:, 2 + 2 * u + t // 2, t % 2 * 2 * P:t % 2 * 2 * P + 2 * P],
                                           xs[:, u * 4 + t, :], winT[:, B0:SM0], start=True, stop=True)
                        T.done(mm, f"x{u}")
                when(pe, A, "z1", NCH - 1)
                when(pe, V, "bc1", rounds - 1)
                for j in range(NT):
                    mm = pe.matmul(k.ps[:, j // 8, (j % 8) * NSM:(j % 8 + 1) * NSM], k.xnT[:, j * P:j * P + P],
                                   winT[:, SM0:], start=True, stop=True)
                T.done(mm, "sm")
                when(pe, V, "adt")
                T.done(pe.matmul(k.ps[:, 4, 0:NT * H2], k.triu[:], flat(L["adt"][:]), start=True, stop=True), "cum")
                T.done(pe.matmul(k.ps[:, 5, 0:NT * H2], k.ones[:], flat(L["adt"][:]), start=True, stop=True), "end")
                when(pe, V, "q")
                pe.matmul(k.ps[:, 6, 0:NT * H2], shift[:], flat(q[:, 0:NT, :]), start=True, stop=False)
                T.done(pe.matmul(k.ps[:, 6, 0:NT * H2], corner[:], flat(q[:, 1:NT + 1, :]), start=False, stop=True), "shift")
                when(pe, V, "ang")
                with pe.Fori(0, CPB) as c:
                    when(pe, A, "th", c - 1)
                    when(pe, G, "run", c - 1)
                    part = ang[:].rearrange("p (b c) n -> p b (c n)", b=B)[:, :, ds(c * H2 * NANG, H2 * NANG)]
                    o = k.ps[:, 0, :].rearrange("p (b n) -> p b n", b=B)
                    pe.matmul(o, k.triu[:], part, start=True, stop=False)
                    T.done(pe.matmul(o, k.ones[:], run[:], start=False, stop=True), "th")

            @block.scalar
            def _(act):
                act.wait_ge(s_w, n_w)
                A.done(act.activation(neg[:], wt[:], ACT.Abs, accum_out=wsum[:, 0:1]), "wabs")
                with act.Fori(0, NCH) as i:
                    for c in range(2):
                        when(act, T, f"z{c}", i)
                        A.done(act.activation(L["zs"][:, c, ds(i * CH, CH)], k.ps[:, c, :], ACT.Silu), f"z{c}")
                with act.Fori(0, rounds) as i:
                    for u in range(2):
                        when(act, T, f"x{u}", i - 1)
                        hold(k, act)
                        A.done(act.copy(flat(xs[:, u * 4:u * 4 + 4, :]), k.xnT[:, ds((i * 8 + u * 4) * P, 4 * P)]), f"xs{u}")
                    for u in range(2):
                        when(act, V, f"bc{u}", i)
                        when(act, V, f"ss{u}", i - 1)
                        hold(k, act)
                        A.done(act.activation(flat(squares[:, u * 8:u * 8 + 8, :]),
                                              flat(L["bc"][:, ds(i * 8 + u * 4, 4), :]), ACT.Square), f"sq{u}")
                when(act, T, "sm")
                for g in range(4):
                    cp = act.copy(sm[:, g * 8:g * 8 + 8, :], k.ps[:, g, 0:8 * NSM].rearrange("p (t n) -> p t n", n=NSM))
                A.done(cp, "sm")
                when(act, V, "ss1", rounds - 1)
                A.done(act.activation(ssq[:], ssq[:], ACT.Sqrt, scale=1.0 / P, bias=k.eps), "rms")
                when(act, V, "nabs")
                A.done(act.activation(t2[:], t2[:], ACT.Exp), "exp")
                when(act, A, "exp")
                A.done(act.activation(t3[:], t2[:], ACT.Ln, bias=k.one), "ln")
                A.done(act.activation(lam[:], sm[:, :, 2 * H2:3 * H2], ACT.Exp, scale=-1.0), "etrap")
                when(act, T, "end")
                A.done(act.activation(L["cend"][:], k.ps[:, 5, 0:NT * H2].rearrange("p (t h) -> p t h", h=H2), ACT.Exp), "eend")
                when(act, V, "wb")
                A.done(act.activation(L["wb"][:], L["wb"][:], ACT.Exp), "ewb")
                with act.Fori(0, CPB) as c:
                    when(act, T, "th", c)
                    o = L["sin"][:].rearrange("p (b c) n -> p b (c n)", b=B)[:, :, ds(c * H2 * NANG, H2 * NANG)]
                    A.done(act.copy(o, k.ps[:, 0, :].rearrange("p (b n) -> p b n", b=B)), "th")
                when(act, V, "clamp")
                A.done(act.activation(L["sin"][:], ang[:], ACT.Sin), "sin")
                A.done(act.activation(turn[:], ang[:], ACT.Abs), "abs")
                when(act, A, "abs")
                A.done(act.activation(L["cos"][:], turn[:], ACT.Sin, scale=-1.0, bias=k.halfpi), "cos")

            @block.vector
            def _(dve):
                def step(ins, name):
                    V.done(ins, name)
                    when(dve, V, name)

                dve.wait_ge(s_w, n_w)
                when(dve, T, "wsum")
                step(dve.tensor_scalar(wsum[:, 1:2], k.ps[:, 7, 0:1], 1.0 / (P * P), 0.7, ALU.mult, ALU.mult), "delta")
                step(dve.tensor_scalar(neg[:], wt[:], -1.0, wsum[:, 1:2], ALU.mult, ALU.is_gt), "pos")
                step(dve.tensor_scalar(wt[:], wt[:], wsum[:, 1:2], None, ALU.is_gt), "neg")
                step(dve.tensor_tensor(wt[:], wt[:], neg[:], ALU.subtract), "tern")
                step(dve.tensor_scalar(L["weff"][:], wt[:], alpha[:], None, ALU.mult), "weff")
                step(dve.tensor_tensor(L["dI"][:], k.ident[:].unsqueeze(1).to_broadcast([P, H2, P]),
                                       dpar[:].unsqueeze(2).to_broadcast([P, H2, P]), ALU.mult), "dI")
                with dve.Fori(0, rounds) as i:
                    for u in range(2):
                        when(dve, T, f"x{u}", i)
                        V.done(dve.tensor_copy(flat(L["bc"][:, ds(i * 8 + u * 4, 4), :]), flat(k.ps[:, 2 + 2 * u:4 + 2 * u, :])),
                               f"bc{u}")
                    for u in range(2):
                        when(dve, A, f"sq{u}", i)
                        V.done(dve.tensor_reduce(flat(ssq[:, ds(i * 8 + u * 4, 4), :]), squares[:, u * 8:u * 8 + 8, :],
                                                 AX_X, ALU.add), f"ss{u}")
                when(dve, A, "rms")
                step(dve.reciprocal(ssq[:], ssq[:]), "rstd")
                when(dve, A, "sm")
                step(dve.tensor_tensor(pre[:, 0], sm[:, :, 0:H2], dtb[:].unsqueeze(1).to_broadcast([P, NT, H2]),
                                       ALU.add), "pre")
                step(dve.tensor_copy(pre[:, 1], sm[:, :, H2:2 * H2]), "preA")
                step(dve.tensor_scalar(t1[:], pre[:], 0.0, None, ALU.max), "relu")
                step(dve.scalar_tensor_tensor(out=flat(t2[:]), in0=flat(pre[:]), scalar=-1.0, in1=flat(pre[:]),
                                              op0=ALU.mult, op1=ALU.min), "nabs")
                when(dve, A, "ln")
                step(dve.tensor_tensor(t1[:], t1[:], t3[:], ALU.add), "sp")
                step(dve.tensor_scalar(t3[:], t2[:], 1.0, None, ALU.add), "u1")
                step(dve.scalar_tensor_tensor(out=flat(t3[:]), in0=flat(t3[:]), scalar=-1.0, in1=flat(t2[:]),
                                              op0=ALU.add, op1=ALU.subtract), "u1b")
                step(dve.tensor_tensor(t1[:], t1[:], t3[:], ALU.subtract), "corr")
                dt = t1[:, 0]
                step(dve.tensor_scalar(t1[:, 1], t1[:, 1], 1e-4, -1.0, ALU.max, ALU.mult), "afloor")
                step(dve.tensor_tensor(L["adt"][:], t1[:, 1], dt, ALU.mult), "adt")
                when(dve, A, "etrap")
                step(dve.tensor_scalar(lam[:], lam[:], 1.0, None, ALU.add), "lam")
                step(dve.reciprocal(lam[:], lam[:]), "lamr")
                step(dve.tensor_tensor(L["wdiag"][:], dt, lam[:], ALU.mult), "wdiag")
                step(dve.tensor_scalar(lam[:], lam[:], -1.0, 1.0, ALU.mult, ALU.add), "qlam")
                when(dve, G, "qz")
                step(dve.tensor_tensor(q[:, 0:NT, :], dt, lam[:], ALU.mult), "q")
                when(dve, T, "shift")
                step(dve.tensor_copy(L["v"][:], k.ps[:, 6, 0:NT * H2].rearrange("p (t h) -> p t h", h=H2)), "v")
                step(dve.tensor_tensor(w1[:], L["v"][:], L["wdiag"][:], ALU.add), "w1")
                step(dve.tensor_copy(L["cum"][:], k.ps[:, 4, 0:NT * H2].rearrange("p (t h) -> p t h", h=H2)), "cum")
                when(dve, A, "eend")
                step(dve.tensor_tensor(L["wb"][:], k.ps[:, 5, 0:NT * H2].rearrange("p (t h) -> p t h", h=H2), L["cum"][:],
                                       ALU.subtract), "wb")
                when(dve, A, "ewb")
                step(dve.tensor_tensor(L["wb"][:], L["wb"][:], w1[:], ALU.mult), "wbe")
                step(dve.tensor_tensor(L["wb"][:], L["wb"][:], keep[:], ALU.mult), "wbk")
                step(dve.tensor_tensor(ang[:].rearrange("p t (h a) -> p t h a", h=H2),
                                       sm[:, :, 3 * H2:].unsqueeze(2).to_broadcast([P, NT, H2, NANG]),
                                       dt.unsqueeze(3).to_broadcast([P, NT, H2, NANG]), ALU.mult), "ang")
                bc4 = L["bc"][:].rearrange("p t (r n) -> p (t r) n", r=2)
                step(dve.tensor_tensor(bc4, bc4, ssq[:].rearrange("p t r -> p (t r)").unsqueeze(2)
                                       .to_broadcast([P, NT * 2, P]), ALU.mult), "bcn")
                step(dve.tensor_tensor(L["bc"][:], L["bc"][:], flat(nw[:]).unsqueeze(1).to_broadcast([P, NT, 2 * P]),
                                       ALU.mult), "bcw")
                when(dve, A, "th", CPB - 1)
                when(dve, T, "th", CPB - 1)
                when(dve, G, "run", CPB - 1)
                th = flat(L["sin"][:])
                step(dve.tensor_scalar(flat(turn[:]), th, float(1 / (2 * np.pi)), ROUND, ALU.mult, ALU.add), "k1")
                step(dve.tensor_scalar(flat(turn[:]), flat(turn[:]), -ROUND, None, ALU.add), "k2")
                for n, (x, c) in enumerate(((th, TURN[0]), (flat(ang[:]), TURN[1]), (flat(ang[:]), TURN[2]))):
                    step(dve.scalar_tensor_tensor(out=flat(ang[:]), in0=flat(turn[:]), scalar=-c, in1=x,
                                                  op0=ALU.mult, op1=ALU.add), f"r{n + 1}")
                lim = 3.1415925
                step(dve.tensor_scalar(flat(ang[:]), flat(ang[:]), lim, -lim, ALU.min, ALU.max), "clamp")

            @block.gpsimd
            def _(pool):
                G.done(pool.memset(q[:, NT:, :], 0.0), "qz")
                G.done(pool.memset(run[:], 0.0), "run0")
                when(pool, V, "ang")
                with pool.Fori(0, CPB) as c:
                    when(pool, T, "th", c)
                    hold(k, pool)
                    part = ang[:].rearrange("p (b c) n -> p b (c n)", b=B)[:, :, ds(c * H2 * NANG, H2 * NANG)]
                    G.done(pool.tensor_tensor(run[:], run[:], part, ALU.add), "run")
                when(pool, A, "eend")
                when(pool, G, "run", CPB - 1)
                pool.wait_ge(s_w, n_w)
                G.done(pool.tensor_tensor(L["cend"][:], L["cend"][:], keep[:], ALU.mult), "cend")
        for s in (A, T, V, G):
            s.close()


def mamba3_chunks_stage(k, L):
    nc = k.nc
    with ExitStack() as ctx:
        sb = lambda x, shape, dt=F32: k.sb("c2_" + x, shape, dt, ctx=ctx)
        xs, xns = sb("x", [P, 2, DI2]), sb("xn", [P, 2, P])
        ta = sb("triu_adt", [P, H2, P])
        bch = sb("bch", [P, 2, 2, H2, P])
        pa, pb, pc, pd = (sb(f"rope{i}", [P, 2, H2, NANG]) for i in range(4))
        wt = sb("wt", [P, 2, H2, P])
        bw = sb("bw", [P, 2, H2, P])
        bF, cF, cFe = sb("bF", [P, H2, P]), sb("cF", [P, H2, P]), sb("cFe", [P, 2, H2, P])
        ebc, arg, E = sb("ebc", [P, 2, H2, P]), sb("arg", [P, H2, P]), sb("E", [P, 2, H2, P])
        M = sb("M", [P, 2, H2, P])
        H, Ht = sb("H", [P, H2, HP]), sb("Ht", [P, H2, HP])
        g = sb("g", [P, 2, 2, P])
        RV, SV = Stream(k, "rope_dve", ["bch", "ab", "n1", "arg"]), Stream(k, "score_dve", ["cFe", "Q", "M"])
        RA, SA = Stream(k, "rope_act", ["ta", "ebc", "E"]), Stream(k, "score_act", ["xn", "bF", "cF", "x"])
        RG, SG = Stream(k, "rope_pool", ["cd", "n2", "wt"]), Stream(k, "score_pool", ["bw"])
        RT, ST = Stream(k, "rope_pe", ["cum"]), Stream(k, "score_pe", ["x", "trB", "trC", "st"])
        BT = Stream(k, "b_pe", ["y", "state", "out"])
        BV = Stream(k, "b_dve", ["g", "H", "x"])
        BG = Stream(k, "b_pool", ["Ht"])
        zero = k.sem("s_H_zero")
        trB, trC, cum, st, yb, xb, outb, stateb = range(8)

        def pipeline(step, eng):
            step(0, None, None, 0)
            step(1, 0, None, 1)
            with eng.Fori(0, NT // 2 - 1) as i:
                for u in range(2):
                    step(i * 2 + (u + 2), i * 2 + (u + 1), i * 2 + u, u)
            step(None, NT - 1, NT - 2, 0)
            step(None, None, NT - 1, 1)

        with nc.Block() as block:
            @block.vector
            def _(dve):
                for stream in (RV, SV, BV):
                    stream.seed(dve)
                dve.memset(H[:], 0.0).then_inc(zero, 1)

                def rotate(c, u):
                    when(dve, ST, "trC", c - 2)
                    when(dve, SG, "bw", c - 2)
                    src = L["bc"][:, ds(c, 1), :].rearrange("p a (r n) -> p (a r) n", r=2)
                    RV.done(dve.tensor_tensor(bch[:, u], src.unsqueeze(2).to_broadcast([P, 2, H2, P]), L["hbias"][:],
                                              ALU.add), "bch")
                    when(dve, RV, "bch", c)
                    v1, v2 = bch[:, u, :, :, 0:NANG], bch[:, u, :, :, NANG:2 * NANG]
                    cos = L["cos"][:, ds(c, 1), :].rearrange("p a (h n) -> p a h n", h=H2).to_broadcast([P, 2, H2, NANG])
                    sin = L["sin"][:, ds(c, 1), :].rearrange("p a (h n) -> p a h n", h=H2).to_broadcast([P, 2, H2, NANG])
                    dve.tensor_tensor(pa[:], v1, cos, ALU.mult)
                    RV.done(dve.tensor_tensor(pb[:], v2, sin, ALU.mult), "ab")
                    when(dve, RG, "cd", c)
                    when(dve, RV, "ab", c)
                    RV.done(dve.tensor_tensor(v1, pa[:], pb[:], ALU.subtract), "n1")

                def argument(c, u):
                    when(dve, RA, "ebc", c)
                    when(dve, RT, "cum", c)
                    for hd in range(H2):
                        a = dve.scalar_tensor_tensor(out=arg[:, hd, :], in0=k.ps[:, cum, hd * P:hd * P + P],
                                                     scalar=L["cum"][:, ds(c, 1), hd], in1=L["maskneg"][:],
                                                     op0=ALU.subtract, op1=ALU.add)
                    RV.done(a, "arg")

                def step(r, s, b, u):
                    if r is not None:
                        rotate(r, u)
                    if s is not None:
                        when(dve, SA, "cF", s)
                        when(dve, RA, "ebc", s)
                        when(dve, BT, "y", s - 2)
                        SV.done(dve.tensor_tensor(cFe[:, 1 - u], cF[:], ebc[:, 1 - u], ALU.mult), "cFe")
                    if r is not None:
                        argument(r, u)
                    if b is not None:
                        when(dve, BT, "y", b)
                        y = k.ps[:, yb, 0:2 * P].rearrange("p (a n) -> p a n", a=2)
                        BV.done(dve.tensor_tensor(g[:, u], y, L["zs"][:, :, ds(b * P, P)], ALU.mult), "g")
                        when(dve, BT, "state", b)
                        when(dve, BG, "Ht", b)
                        BV.done(dve.tensor_tensor(H[:], Ht[:], k.ps[:, stateb, 0:DI2].rearrange("p (h n) -> p h n", h=H2),
                                                  ALU.add), "H")
                    if s is not None:
                        when(dve, ST, "st", s)
                        when(dve, RA, "E", s)
                        SV.done(dve.tensor_tensor(flat(M[:, 1 - u]), k.ps[:, st, :], flat(E[:, 1 - u]), ALU.mult), "Q")
                        when(dve, SV, "Q", s)
                        when(dve, RG, "wt", s)
                        SV.done(dve.tensor_tensor(M[:, 1 - u], M[:, 1 - u], wt[:, 1 - u], ALU.mult), "M")
                    if b is not None:
                        when(dve, BT, "out", b)
                        x = k.x_tm[:, ds(b, 1), :].rearrange("p a n -> p (a n)")
                        BV.done(dve.tensor_tensor(x, x, k.ps[:, outb, 0:D], ALU.add), "x")

                pipeline(step, dve)

            @block.gpsimd
            def _(pool):
                for stream in (RG, SG, BG):
                    stream.seed(pool)
                full = [P, H2, P]

                def step(r, s, b, u):
                    wide = lambda x, c: x[:, ds(c, 1), :].rearrange("p a h -> p (a h)").unsqueeze(2).to_broadcast(full)
                    if b is not None:
                        when(pool, BV, "H", b - 1)
                        hold(k, pool)
                        ce = L["cend"][:, ds(b, 1), :].rearrange("p a h -> p (a h)").unsqueeze(2).to_broadcast([P, H2, HP])
                        BG.done(pool.tensor_tensor(Ht[:], H[:], ce, ALU.mult), "Ht")
                    if r is not None:
                        when(pool, RV, "bch", r)
                        when(pool, RG, "n2", r - 1)
                        hold(k, pool)
                        v1, v2 = bch[:, u, :, :, 0:NANG], bch[:, u, :, :, NANG:2 * NANG]
                        cos = L["cos"][:, ds(r, 1), :].rearrange("p a (h n) -> p a h n", h=H2).to_broadcast([P, 2, H2, NANG])
                        sin = L["sin"][:, ds(r, 1), :].rearrange("p a (h n) -> p a h n", h=H2).to_broadcast([P, 2, H2, NANG])
                        pool.tensor_tensor(pc[:], v1, sin, ALU.mult)
                        RG.done(pool.tensor_tensor(pd[:], v2, cos, ALU.mult), "cd")
                        when(pool, RV, "ab", r)
                        when(pool, RG, "cd", r)
                        RG.done(pool.tensor_tensor(v2, pc[:], pd[:], ALU.add), "n2")
                    if s is not None:
                        when(pool, RV, "n1", s)
                        when(pool, RG, "n2", s)
                        when(pool, BT, "state", s - 2)
                        hold(k, pool)
                        SG.done(pool.tensor_tensor(bw[:, 1 - u], bch[:, 1 - u, 0], wide(L["wb"], s), ALU.mult), "bw")
                    if r is not None:
                        when(pool, SV, "M", r - 2)
                        hold(k, pool)
                        pool.tensor_tensor(wt[:, u], L["strict"][:].unsqueeze(1).to_broadcast(full), wide(L["v"], r),
                                           ALU.mult).then_inc(k.wt_half, 1)
                        pool.wait_ge(k.wt_half, r + 1)
                        hold(k, pool)
                        RG.done(pool.tensor_tensor(wt[:, u], wt[:, u], wide(L["wdiag"], r), ALU.add), "wt")

                pool.wait_ge(zero, 1)
                pipeline(step, pool)

            @block.scalar
            def _(act):
                for stream in (RA, SA):
                    stream.seed(act)

                def step(r, s, b, u):
                    if s is not None:
                        when(act, BT, "out", s - 2)
                        SA.done(act.copy(xns[:, 1 - u, :], k.xnT[:, ds(s * P, P)]), "xn")
                    if r is not None:
                        when(act, RT, "cum", r - 1)
                        for hd in range(H2):
                            t = act.activation(ta[:, hd, :], k.triu[:], ACT.Copy, scale=L["adt"][:, ds(r, 1), hd])
                        RA.done(t, "ta")
                    if s is not None:
                        when(act, ST, "trB", s)
                        when(act, ST, "st", s - 1)
                        SA.done(act.copy(flat(bF[:]), k.ps[:, trB, :]), "bF")
                        when(act, ST, "trC", s)
                        when(act, SV, "cFe", s - 1)
                        SA.done(act.copy(flat(cF[:]), k.ps[:, trC, :]), "cF")
                        SA.done(act.copy(xs[:, 1 - u, :], k.ps[:, xb, 0:DI2]), "x")
                    if r is not None:
                        when(act, RT, "cum", r)
                        when(act, SV, "cFe", r - 2)
                        RA.done(act.activation(flat(ebc[:, u]), k.ps[:, cum, :], ACT.Exp), "ebc")
                        when(act, RV, "arg", r)
                        when(act, SV, "Q", r - 2)
                        RA.done(act.activation(E[:, u], arg[:], ACT.Exp), "E")

                pipeline(step, act)

            @block.tensor
            def _(pe):
                for stream in (RT, ST, BT):
                    stream.seed(pe)

                def step(r, s, b, u):
                    if r is not None:
                        when(pe, RA, "ta", r)
                        when(pe, RV, "arg", r - 1)
                        RT.done(pe.matmul(k.ps[:, cum, :], k.ones[:], flat(ta[:]), start=True, stop=True), "cum")
                    if s is not None:
                        when(pe, SA, "xn", s)
                        when(pe, RV, "n1", s)
                        when(pe, RG, "n2", s)
                        ST.done(pe.matmul(k.ps[:, xb, 0:DI2], xns[:, 1 - u, :], L["winT"][:, X0:B0], start=True, stop=True),
                                "x")
                        for q, (bank, name) in enumerate(((trB, "trB"), (trC, "trC"))):
                            for hd in range(H2):
                                t = pe.transpose(k.ps[:, bank, hd * P:hd * P + P], bch[:, 1 - u, q, hd, :], k.ident[:])
                            ST.done(t, name)
                    if b is not None:
                        when(pe, SV, "M", b)
                        when(pe, SA, "x", b)
                        when(pe, BV, "H", b - 1)
                        for hd in range(H2):
                            o = k.ps[HP * (hd % 2):HP * (hd % 2) + HP, yb, (hd // 2) * P:(hd // 2) * P + P]
                            x = xs[:, u, hd * HP:hd * HP + HP]
                            pe.matmul(o, x, M[:, u, hd, :], start=True, stop=False)
                            pe.matmul(o, x, L["dI"][:, hd, :], start=False, stop=False)
                            t = pe.matmul(o, H[:, hd, :], cFe[:, u, hd, :], start=False, stop=True)
                        BT.done(t, "y")
                        when(pe, SG, "bw", b)
                        for hd in range(H2):
                            t = pe.matmul(k.ps[:, stateb, hd * HP:hd * HP + HP], bw[:, u, hd, :],
                                          xs[:, u, hd * HP:hd * HP + HP], start=True, stop=True)
                        BT.done(t, "state")
                    if s is not None:
                        when(pe, SA, "cF", s)
                        when(pe, SV, "Q", s - 1)
                        for hd in range(H2):
                            t = pe.matmul(k.ps[:, st, hd * P:hd * P + P], bF[:, hd, :], cF[:, hd, :], start=True, stop=True)
                        ST.done(t, "st")
                    if b is not None:
                        o = k.ps[:, outb, 0:D]
                        when(pe, BV, "x", b - 1)
                        pe.matmul(o, k.ones[0:1, :], L["bias"][:], start=True, stop=False)
                        pe.matmul(o, xns[:, u, :], L["weff"][:], start=False, stop=False)
                        when(pe, BV, "g", b)
                        for q in range(2):
                            t = pe.matmul(o, g[:, u, q, :], L["woutT"][:, q, :], start=False, stop=q == 1)
                        BT.done(t, "out")

                pe.wait_ge(zero, 1)
                pipeline(step, pe)


def layer2(k):
    norm_stage(k, "n2", k.x_tm, to_xnT(k))
    with ExitStack() as ctx:
        sb = lambda x, shape, dt=F32: k.sb("l2_" + x, shape, dt, ctx=ctx)
        L = {x: sb(x, [P, NT, H2]) for x in ("adt", "cum", "wdiag", "v", "wb", "cend")}
        L.update(winT=sb("winT", [P, SM0 + NSM]), woutT=sb("woutT", [P, 2, D]), weff=sb("weff", [P, D]),
                 dI=sb("dI", [P, H2, P]), hbias=sb("hbias", [P, 2, H2, P]), bias=sb("bias", [1, D]),
                 maskneg=sb("maskneg", [P, P]), strict=sb("strict", [P, P]),
                 zs=sb("zs", [P, 2, TOK]), bc=sb("bc", [P, NT, 2 * P]),
                 sin=sb("sin", [P, NT, H2 * NANG]), cos=sb("cos", [P, NT, H2 * NANG]))
        mamba3_gates_stage(k, L)
        k.wt_half = k.sem("c2_wt_half")
        mamba3_chunks_stage(k, L)


GH = 4
NG = HEADS // GH
NI = B * NG
QT = S // P
COMBO_Q = (0, 1, 2, 0, 1, 0)
COMBO_K = (0, 0, 0, 1, 1, 2)
NCMB = len(COMBO_Q)
RUNS = ((0, 3), (3, 2), (5, 1))
KROWS = NCMB * HD
TILES = [(qc, kt) for qc in range(S // CH) for kt in range((qc + 1) * CH // P)]


def attn3_project_stage(k, R):
    nc, ins = k.nc, k.ins
    with ExitStack() as ctx:
        sb = lambda x, shape, dt=F32: k.sb("p3_" + x, shape, dt, ctx=ctx)
        w, bcol, bv = sb("w", [P, 3, P]), sb("bias", [P, 2]), sb("bias_v", [P, P])
        f, r = sb("f", [P, 2, S]), sb("r", [P, 2, S])
        part = [sb(f"part{n}", [P, 3, S], BF16) for n in range(2)]
        xs = sb("x", [P, S])
        s_w = k.sem("s_p3_weights")
        s_st = [k.sem(f"s_p3_store{n}") for n in range(2)]
        T = Steps(k, "pe", [(B, ["q", "k", "v"])])
        A = Steps(k, "act", ["one", (B, ["fq", "fk", "hiq", "hik", "xs", "midq", "midk", "loq", "lok"])])
        V = Steps(k, "dve", ["bq", (B, ["rq", "rk", "rrq", "rrk", "v0", "v1"])])
        wide = lambda ap: ap.rearrange("p a n -> p (a n)")
        with nc.Block() as block:
            @block.sync
            def _(sp):
                sp.dma_start(w[:], ins["L3a_wqkv"]).then_inc(s_w, 16)
                with nc.allow_non_contiguous_dma(reason="two columns"):
                    sp.dma_start(bcol[:], ins["L3a_bqkv"][0:2, :].rearrange("r p -> p r")).then_inc(s_w, 16)
                sp.dma_start(bv[:], ins["L3a_bqkv"][2, :].partition_broadcast(P)).then_inc(s_w, 16)
                with sp.Fori(0, B) as b:
                    for n, x in enumerate("qk"):
                        when(sp, A, f"lo{x}", b)
                        for c in range(3):
                            dst = R["qk"][n, ds(b * NG, NG), c].rearrange("g d h s -> g (d h) s")
                            sp.dma_start(dst, part[n][:, c, :]).then_inc(s_st[n], 16)
                for n in range(2):
                    sp.wait_ge(s_st[n], 48 * B + 16)

            @block.tensor
            def _(pe):
                pe.wait_ge(s_w, 48)
                with pe.Fori(0, B) as b:
                    for n, x in enumerate("qk"):
                        when(pe, A, f"f{x}", b - 1)
                        for t in range(2):
                            mm = pe.matmul(k.ps[:, 2 * n + t, :], w[:, n, :], k.xnT[:, ds(b * S + t * CH, CH)],
                                           start=True, stop=True)
                        T.done(mm, x)
                    when(pe, A, "xs", b)
                    when(pe, V, "v1", b - 1)
                    for t in range(QT):
                        mm = pe.matmul(k.ps[:, 4 + t // 4, t % 4 * P:t % 4 * P + P], xs[:, t * P:t * P + P], w[:, 2, :],
                                       start=True, stop=True)
                    T.done(mm, "v")

            @block.scalar
            def _(act):
                act.wait_ge(s_w, 48)
                for n in range(2):
                    act.sem_inc(s_st[n], 16)
                A.done(act.copy(bcol[:, 1:2], bcol[:, 1:2]), "one")
                when(act, V, "bq")
                with act.Fori(0, B) as b:
                    for n, x in enumerate("qk"):
                        when(act, T, x, b)
                        when(act, V, f"r{x}", b - 1)
                        A.done(act.activation(f[:, n, :], wide(k.ps[:, 2 * n:2 * n + 2, :]), ACT.Identity,
                                              bias=bcol[:, n:n + 1], scale=(float(HD) ** -0.5, 1.0)[n]), f"f{x}")
                    for n, x in enumerate("qk"):
                        when(act, A, f"f{x}", b)
                        act.wait_ge(s_st[n], b * 48 + 16)
                        A.done(act.copy(part[n][:, 0, :], f[:, n, :]), f"hi{x}")
                    when(act, T, "v", b - 1)
                    hold(k, act)
                    A.done(act.copy(xs[:], k.xnT[:, ds(b * S, S)]), "xs")
                    for c, (name, src) in enumerate((("mid", "r"), ("lo", "rr"))):
                        for n, x in enumerate("qk"):
                            when(act, V, f"{src}{x}", b)
                            A.done(act.copy(part[n][:, 1 + c, :], r[:, n, :]), f"{name}{x}")

            @block.vector
            def _(dve):
                dve.wait_ge(s_w, 48)
                when(dve, A, "one")
                V.done(dve.tensor_scalar(bcol[:, 0:1], bcol[:, 0:1], float(HD) ** -0.5, None, ALU.mult), "bq")
                with dve.Fori(0, B) as b:
                    for n, x in enumerate("qk"):
                        when(dve, A, f"hi{x}", b)
                        V.done(dve.tensor_tensor(r[:, n, :], f[:, n, :], part[n][:, 0, :], ALU.subtract), f"r{x}")
                    for n, x in enumerate("qk"):
                        when(dve, A, f"mid{x}", b)
                        V.done(dve.tensor_tensor(r[:, n, :], r[:, n, :], part[n][:, 1, :], ALU.subtract), f"rr{x}")
                    when(dve, T, "v", b)
                    for t in range(2):
                        o = R["v"][:, ds(b * NG, NG), t * 4:t * 4 + 4, :].rearrange("p g t n -> p t g n")
                        V.done(dve.tensor_tensor(o, k.ps[:, 4 + t, :].rearrange("p (t g n) -> p t g n", t=4, g=NG),
                                                 bv[:].rearrange("p (g n) -> p g n", g=NG).unsqueeze(1)
                                                 .to_broadcast([P, 4, NG, GH * HD]), ALU.add), f"v{t}")
        for s in (T, A, V):
            s.close()


def attn3_stage(k, R):
    nc = k.nc
    with ExitStack() as ctx:
        sb = lambda x, shape, dt=F32: k.sb("a3_" + x, shape, dt, ctx=ctx)
        qs = [sb(f"q_stack{u}", [P, GH, S], BF16) for u in range(2)]
        kst = [sb(f"k_stack{u}", [P, GH, S], BF16) for u in range(2)]
        consts, constsb = sb("consts", [P, 3, P]), sb("consts_bf16", [P, 3, P], BF16)
        identb, maskq, maskk = (constsb[:, n, :] for n in range(3))
        vp = sb("v_padded", [P, 2, QT, GH, 32])
        m = sb("m", [P, GH, QT])
        mT, mr = sb("mT", [32, P]), sb("mr", [32, P])
        mp = sb("m_parts", [32, 3, P], BF16)
        pT = sb("pT", [P, 2, GH, CH])
        oT = sb("oT", [P, 2, CH])
        rs = sb("rs", [P, 4, GH])
        NSU, NTU, GROUPS = QT * GH, len(TILES) * GH, len(TILES)
        FRONT = (0, 8, 8, 4, 4, 4, 4)
        assert sum(FRONT) == NSU
        s_c = k.sem("s_a3_consts")
        s_qk = [k.sem(f"s_a3_stacks{u}") for u in range(2)]
        s_m = [k.sem(f"s_a3_max{u}") for u in range(2)]
        FP = Stream(k, "a3_f_pe", [f"S{n}" for n in range(NSU)] + ["mT"])
        FV = Stream(k, "a3_f_dve", [f"m{n}" for n in range(NSU)] + ["mT", "hi", "r", "mid", "rr", "lo"])
        FG = Stream(k, "a3_f_pool", ["v"])
        BP = Stream(k, "a3_b_pe", [f"T{n}" for n in range(NTU)])
        BO = Stream(k, "a3_b_sums", [f"O{g}" for g in range(GROUPS // 2 - 1)] + ["tr0"]
                    + [f"O{g}" for g in range(GROUPS // 2 - 1, GROUPS)] + ["tr1"])
        BA = Stream(k, "a3_b_act", [x for n in range(NTU) for x in [f"e{n}"] + {3: ["o1"], 19: ["o0"]}.get(n, [])])
        BV = Stream(k, "a3_b_dve", ["rs0", "n0", "rs1", "n1"])
        zeroed = k.sem("a3_zeroed")
        bankS, bankT, bankO, bankX = 0, 4, 6, 7

        with nc.Block() as block:
            @block.sync
            def _(sp):
                for n, src in enumerate(("ident", "maskneg_q", "maskneg")):
                    sp.dma_start(consts[:, n, :], k.ins[src]).then_inc(s_c, 16)
                sp.wait_ge(zeroed, 4)

                def stacks(c, u):
                    when(sp, BP, f"T{NTU - 1}", c - 2)
                    for r, w in RUNS:
                        q = R["qk"][0, ds(c, 1), 0:w].rearrange("a c d h s -> (a c d) (h s)")
                        kk = R["qk"][1, ds(c, 1), COMBO_K[r]].rearrange("a d h s -> (a d) (h s)")
                        sp.dma_start(qs[u][r * HD:(r + w) * HD].rearrange("p h s -> p (h s)"), q).then_inc(s_qk[u], 16)
                        sp.dma_start(kst[u][r * HD:(r + w) * HD].rearrange("p h s -> p (h s)"),
                                     kk.unsqueeze(0).to_broadcast([w, HD, GH * S])).then_inc(s_qk[u], 16)

                def maxima(c, u):
                    when(sp, FV, "lo", c)
                    for n in range(3):
                        sp.dma_start(qs[u][KROWS + n:KROWS + n + 1, :, :].rearrange("a h (t q) -> a (h t) q", q=P),
                                     mp[:, n, :]).then_inc(s_m[u], 16)

                stacks(0, 0)
                stacks(1, 1)
                maxima(0, 0)
                with sp.Fori(0, NI // 2 - 1) as i:
                    maxima(i * 2 + 1, 1)
                    stacks(i * 2 + 2, 0)
                    maxima(i * 2 + 2, 0)
                    stacks(i * 2 + 3, 1)
                maxima(NI - 1, 1)
                sp.wait_ge(s_c, 48)
                for u in range(2):
                    sp.wait_ge(s_qk[u], 16 * 2 * len(RUNS) * NI // 2)
                    sp.wait_ge(s_m[u], 16 * 3 * NI // 2 + 16)

            def half(c, u):
                return c // 2 if isinstance(c, int) else (c - u) // 2

            @block.tensor
            def _(pe):
                FP.seed(pe)
                BP.seed(pe)
                BO.seed(pe)
                pe.wait_ge(zeroed, 5)

                def score(c, u, i2, n):
                    t, h = n // GH, n % GH
                    if n == 0:
                        pe.wait_ge(s_qk[u], (i2 + 1) * (16 * 2 * len(RUNS)))
                    if n >= 2:
                        when(pe, FV, f"m{n - 2}", c)
                    else:
                        when(pe, FV, f"m{NSU - 2 + n}", c - 1)
                    bank = bankS + 2 * (n % 2)
                    for x in range(0, (t + 1) * P, CH):
                        w = min(CH, (t + 1) * P - x)
                        diag = x + w == (t + 1) * P
                        plain = w - P if diag else w
                        q_ = qs[u][0:KROWS, h, t * P:t * P + P]
                        if plain:
                            mm = pe.matmul(k.ps[:, bank + x // CH, 0:plain], q_, kst[u][0:KROWS, h, x:x + plain],
                                           start=True, stop=True)
                        if diag:
                            o = k.ps[:, bank + x // CH, plain:w]
                            pe.matmul(o, q_, kst[u][0:KROWS, h, x + plain:x + w], start=True, stop=False)
                            mm = pe.matmul(o, identb, maskq, start=False, stop=True)
                    FP.done(mm, f"S{n}")

                def turn_max(c, u):
                    when(pe, FV, f"m{NSU - 1}", c)
                    when(pe, BV, "n0", c - 1)
                    FP.done(pe.transpose(k.ps[0:32, bankX, 0:P], m[:].rearrange("p h t -> p (h t)"), k.ident[:]), "mT")

                def tile(n):
                    qc, kt = TILES[n // GH]
                    q0 = max(qc * CH, kt * P)
                    return qc, kt, n % GH, q0, (qc + 1) * CH - q0

                def scoreT(c, u, i2, n):
                    qc, kt, h, q0, w = tile(n)
                    if n == 0:
                        pe.wait_ge(s_m[u], (i2 + 1) * (16 * 3) + 16)
                    if n >= 2:
                        when(pe, BA, f"e{n - 2}", c)
                    else:
                        when(pe, BA, f"e{NTU - 2 + n}", c - 1)
                    x = P if kt * P >= qc * CH else 0
                    k_, rows = kst[u][0:KROWS + 3, h, kt * P:kt * P + P], slice(0, KROWS + 3)
                    if w > x:
                        mm = pe.matmul(k.ps[:, bankT + n % 2, x:w], k_, qs[u][rows, h, q0 + x:q0 + w], start=True, stop=True)
                    if x:
                        o = k.ps[:, bankT + n % 2, 0:x]
                        pe.matmul(o, k_, qs[u][rows, h, q0:q0 + x], start=True, stop=False)
                        mm = pe.matmul(o, identb, maskk, start=False, stop=True)
                    BP.done(mm, f"T{n}")

                def sums(c, u, g, h):
                    qc, kt, _, q0, w = tile(GH * g)
                    if h == 0:
                        if g == 0:
                            when(pe, FG, "v", c)
                        if g == 0:
                            when(pe, BA, "o1", c)
                        elif g == 4:
                            when(pe, BA, "o0", c)
                        else:
                            when(pe, BA, f"e{GH * g + GH - 1}", c)
                    mm = pe.matmul(k.ps[32 * h:32 * h + 32, bankO, CH - w:CH], vp[:, u, kt, h, :],
                                   pT[:, g % 2, h, 0:w], start=kt == 0, stop=kt * P >= qc * CH, skip_group_check=True)
                    if h == GH - 1:
                        BO.done(mm, f"O{g}")

                def turn_sums(c, qc, last=False):
                    when(pe, BA, f"o{qc}", c + qc)
                    if qc == 0:
                        when(pe, BV, "n1", c - 1)
                    elif last:
                        when(pe, BV, "n0", c)
                    else:
                        when(pe, FV, "mT", c + 1)
                    for t in range(4):
                        mm = pe.transpose(k.ps[:, bankX, t * P:t * P + P], oT[:, qc, t * P:t * P + P], k.ident[:])
                    BO.done(mm, f"tr{qc}")

                def item(front, back):
                    units = iter(range(NSU) if front else ())
                    for g in range(GROUPS if back else len(FRONT)):
                        share = FRONT[g] // GH if g < len(FRONT) else 0
                        if back:
                            c, u = back[0], back[1]
                            first = isinstance(c, int) and c == 0
                            if g == 1 and not first:
                                turn_sums(c - 1, 1)
                        for h in range(GH):
                            if back:
                                scoreT(*back, GH * g + h)
                            for f in range(share if front else 0):
                                score(*front, next(units))
                            if back and g > 0:
                                sums(c, u, g - 1, h)
                            elif back and not first:
                                sums(c - 1, 1 - u, GROUPS - 1, h)
                        if back and g == GROUPS // 2 - 1:
                            turn_sums(c, 0)
                        if front and g == (len(FRONT) if back else len(FRONT) - 1):
                            turn_max(front[0], front[1])

                item((0, 0, 0), None)
                item((1, 1, 0), (0, 0, 0))
                with pe.Fori(0, NI // 2 - 1) as i:
                    item((i * 2 + 2, 0, i + 1), (i * 2 + 1, 1, i))
                    item((i * 2 + 3, 1, i + 1), (i * 2 + 2, 0, i + 1))
                item(None, (NI - 1, 1, NI // 2 - 1))
                for h in range(GH):
                    sums(NI - 1, 1, GROUPS - 1, h)
                turn_sums(NI - 1, 1, last=True)

            @block.scalar
            def _(act):
                BA.seed(act)

                def out(c, half):
                    when(act, BO, f"O{(3, GROUPS - 1)[half]}", c)
                    when(act, BO, f"tr{half}", c - 1)
                    BA.done(act.copy(oT[:, half, :], k.ps[:, bankO, :]), f"o{half}")

                def back(c, first=False):
                    for n in range(NTU):
                        g = n // GH
                        w = (TILES[g][0] + 1) * CH - max(TILES[g][0] * CH, TILES[g][1] * P)
                        when(act, BP, f"T{n}", c)
                        if n % GH == 0:
                            if g >= 2:
                                when(act, BO, f"O{g - 2}", c)
                            else:
                                when(act, BO, f"O{GROUPS - 2 + g}", c - 1)
                        BA.done(act.activation(pT[:, g % 2, n % GH, 0:w], k.ps[:, bankT + n % 2, 0:w], ACT.Exp), f"e{n}")
                        if n == 3 and first:
                            when(act, BA, "e3", 0)
                            BA.done(act.nop(), "o1")
                        elif n == 3:
                            out(c - 1, 1)
                        if n == 19:
                            out(c, 0)

                back(0, first=True)
                with act.Fori(1, NI) as c:
                    back(c)
                when(act, BO, f"O{GROUPS - 1}", NI - 1)
                when(act, BO, "tr1", NI - 2)
                act.copy(oT[:, 1, :], k.ps[:, bankO, :]).then_inc(BA.sem, GH + 1)

            @block.vector
            def _(dve):
                FV.seed(dve)
                BV.seed(dve)
                for u in range(2):
                    dve.sem_inc(s_m[u], 16)

                def front(c, u, i2, before=None):
                    for n in range(NSU):
                        t, h = n // GH, n % GH
                        when(dve, FP, f"S{n}", c)
                        if n == 0:
                            when(dve, FP, "mT", c - 1)
                        bank = bankS + 2 * (n % 2)
                        src = k.ps[:, bank:bank + 2, :].rearrange("p a n -> p (a n)")[:, 0:(t + 1) * P]
                        FV.done(dve.tensor_reduce(m[:, h, t:t + 1], src, AX_X, ALU.max), f"m{n}")
                        if n == 0 and before is not None and not (isinstance(before, int) and before == 0):
                            back(before - 1, 1)
                        if n == 27 and before is not None:
                            back(before, 0)
                    when(dve, FP, "mT", c)
                    FV.done(dve.tensor_scalar(mT[:], k.ps[0:32, bankX, 0:P], -1.0, None, ALU.mult), "mT")
                    when(dve, FV, "mT", c)
                    dve.wait_ge(s_m[1 - u], (i2 + u) * (16 * 3) + 16)
                    FV.done(dve.tensor_copy(mp[:, 0, :], mT[:]), "hi")
                    when(dve, FV, "hi", c)
                    FV.done(dve.tensor_tensor(mr[:], mT[:], mp[:, 0, :], ALU.subtract), "r")
                    when(dve, FV, "r", c)
                    FV.done(dve.tensor_copy(mp[:, 1, :], mr[:]), "mid")
                    when(dve, FV, "mid", c)
                    FV.done(dve.tensor_tensor(mr[:], mr[:], mp[:, 1, :], ALU.subtract), "rr")
                    when(dve, FV, "rr", c)
                    FV.done(dve.tensor_copy(mp[:, 2, :], mr[:]), "lo")

                def back(c, qc):
                    when(dve, BO, f"tr{qc}", c)
                    o = k.ps[:, bankX, :].rearrange("p (t h n) -> p t h n", t=4, h=GH)
                    BV.done(dve.reciprocal(rs[:], o[:, :, :, HD]), f"rs{qc}")
                    when(dve, BV, f"rs{qc}", c)
                    dst = R["att"][:, ds(c, 1), qc * 4:qc * 4 + 4, :].rearrange("p a t (h n) -> p (a t) h n", h=GH)
                    BV.done(dve.tensor_tensor(dst, o[:, :, :, 0:HD], rs[:].unsqueeze(3).to_broadcast([P, 4, GH, HD]),
                                              ALU.mult), f"n{qc}")

                front(0, 0, 0)
                front(1, 1, 0, before=0)
                with dve.Fori(0, NI // 2 - 1) as i:
                    front(i * 2 + 2, 0, i + 1, before=i * 2 + 1)
                    front(i * 2 + 3, 1, i + 1, before=i * 2 + 2)
                back(NI - 2, 1)
                back(NI - 1, 0)
                back(NI - 1, 1)

            @block.gpsimd
            def _(pool):
                FG.seed(pool)
                for u in range(2):
                    pool.memset(kst[u][32:64, :, :], 1.0).then_inc(zeroed, 1)
                pool.wait_ge(zeroed, 2)
                pool.memset(vp[:], 0.0).then_inc(zeroed, 1)
                pool.wait_ge(zeroed, 3)
                pool.memset(vp[:, :, :, :, HD:HD + 1], 1.0).then_inc(zeroed, 1)
                pool.wait_ge(zeroed, 4)
                pool.wait_ge(s_c, 48)
                pool.tensor_copy(constsb[:], consts[:]).then_inc(zeroed, 1)

                with pool.Fori(0, NI // 2) as i:
                    for u in range(2):
                        c = i * 2 + u
                        when(pool, BO, f"O{GROUPS - 1}", c - 2)
                        hold(k, pool)
                        FG.done(pool.tensor_copy(vp[:, u, :, :, 0:HD],
                                                 R["v"][:, ds(c, 1), :, :].rearrange("p a t (h n) -> p (a t) h n", h=GH)), "v")


def attn3_out_stage(k, R):
    nc, ins = k.nc, k.ins
    rounds = NT // 4
    with ExitStack() as ctx:
        sb = lambda x, shape, dt=F32: k.sb("o3_" + x, shape, dt, ctx=ctx)
        w, bias = sb("w", [P, D]), sb("bias", [1, D])
        slot, aT = sb("slot", [P, 4, P]), sb("aT", [P, 4 * P])
        s_w = k.sem("s_o3_weights")
        G = Steps(k, "pool", [(B, ["slot0", "slot1"])])
        T = Steps(k, "pe", [(B, ["tr0", "y0", "tr1", "y1"])])
        A = Steps(k, "act", [(B, ["aT0", "aT1"])])
        V = Steps(k, "dve", [(B, ["x0", "x1"])])
        with nc.Block() as block:
            @block.sync
            def _(sp):
                sp.dma_start(w[:], ins["L3a_wout"]).then_inc(s_w, 16)
                sp.dma_start(bias[:], ins["L3a_bout"].rearrange("(a n) -> a n", a=1)).then_inc(s_w, 16)
                sp.wait_ge(s_w, 32)

            @block.gpsimd
            def _(pool):
                with pool.Fori(0, B) as b:
                    for u in range(2):
                        when(pool, T, f"tr{1 - u}", b - (1 - u))
                        hold(k, pool)
                        src = R["att"][:, ds(b * NG, NG), u * 4:u * 4 + 4, :].rearrange("p g t n -> p t g n")
                        G.done(pool.tensor_copy(slot[:].rearrange("p t (g n) -> p t g n", g=NG), src), f"slot{u}")

            @block.tensor
            def _(pe):
                pe.wait_ge(s_w, 32)
                with pe.Fori(0, B) as b:
                    for u in range(2):
                        when(pe, G, f"slot{u}", b)
                        when(pe, A, f"aT{1 - u}", b - (1 - u))
                        for t in range(4):
                            mm = pe.transpose(k.ps[:, 0, t * P:t * P + P], slot[:, t, :], k.ident[:])
                        T.done(mm, f"tr{u}")
                        when(pe, A, f"aT{u}", b)
                        when(pe, V, f"x{u}", b - 1)
                        for t in range(4):
                            o = k.ps[:, 1 + u, t * P:t * P + P]
                            pe.matmul(o, k.ones[0:1, :], bias[:], start=True, stop=False)
                            mm = pe.matmul(o, aT[:, t * P:t * P + P], w[:], start=False, stop=True)
                        T.done(mm, f"y{u}")

            @block.scalar
            def _(act):
                with act.Fori(0, B) as b:
                    for u in range(2):
                        when(act, T, f"tr{u}", b)
                        when(act, T, f"y{1 - u}", b - (1 - u))
                        A.done(act.copy(aT[:], k.ps[:, 0, :]), f"aT{u}")

            @block.vector
            def _(dve):
                with dve.Fori(0, B) as b:
                    for u in range(2):
                        when(dve, T, f"y{u}", b)
                        x = k.x_tm[:, ds(b * 8 + u * 4, 4), :]
                        V.done(dve.tensor_tensor(x, x, k.ps[:, 1 + u, :].rearrange("p (t d) -> p t d", d=D), ALU.add), f"x{u}")
        for s in (G, T, A, V):
            s.close()


def moe3_stage(k):
    nc, ins = k.nc, k.ins
    rounds = NE // 2
    with ExitStack() as ctx:
        sb = lambda x, shape, dt=F32: k.sb("e3_" + x, shape, dt, ctx=ctx)
        gw, iota = sb("router", [P, NE]), sb("iota", [P, NE])
        pr, work, hot, m = sb("prob", [P, NT, NE]), sb("work", [P, 2, NT, NE]), sb("hot", [P, 2, NT, NE]), sb("m", [P, 3, NT])
        cw, den = sb("cw", [P, NT, NE]), sb("den", [P, NT])
        cT = sb("cwT", [NE, 2, 4 * P])
        w1, w2 = sb("w1", [P, 2, DFF]), sb("w2", [P, 2, FT, D])
        b1, b2 = sb("b1", [P, 2, FT]), sb("b2", [NE, D])
        h = sb("h", [P, 2, FT, CH])
        s_b = k.sem("s_e3_biases")
        s_w = [k.sem(f"s_e3_weights{u}") for u in range(2)]
        pairs = NCH // 2
        T = Steps(k, "pe", ["gate", (pairs, ["cT0", "b0", "cT1", "b1"])])
        A = Steps(k, "act", ["exp", (pairs, ["cT0", "cT1"])])
        V = Steps(k, "dve", ["max", "less", "sum", "rsum", "prob"] + top2_names("r")
                  + ["two", "eps", "rden", "hots", "picked", "cw", (pairs, ["b0", "b1"])])
        up = Count(k, "e3_hidden_tiles", credit=2 * FT)
        act_ = Count(k, "e3_gelu", credit=2 * FT)
        down = Count(k, "e3_down", credit=NCH)
        add = Count(k, "e3_added", credit=2)
        with nc.Block() as block:
            @block.sync
            def _(sp):
                for dst, src in ((b2[:], ins["L3f_b2"]), (gw[:], ins["L3f_routerT"]),
                                 (iota[:], ins["iota"].partition_broadcast(P))):
                    sp.dma_start(dst, src).then_inc(s_b, 16)
                with sp.Fori(0, rounds) as i:
                    for u in range(2):
                        sp.wait_ge(down.sem, down.at((i * 2 + u - 1) * NCH - 1))
                        sp.dma_start(w1[:, u, :], ins["L3f_w1T"][:, ds(i * 2 + u, 1), :].rearrange("p a n -> p (a n)"))\
                          .then_inc(s_w[u], 16)
                        sp.dma_start(w2[:, u, :, :], ins["L3f_w2T"][:, ds(i * 2 + u, 1), :, :]
                                     .rearrange("p a t n -> p (a t) n")).then_inc(s_w[u], 16)
                        sp.dma_start(b1[:, u, :], ins["L3f_b1T"][:, ds(i * 2 + u, 1), :].rearrange("p a t -> p (a t)"))\
                          .then_inc(s_w[u], 16)
                sp.wait_ge(s_b, 48)
                for u in range(2):
                    sp.wait_ge(s_w[u], 48 * rounds)

            @block.tensor
            def _(pe):
                up.seed(pe)
                down.seed(pe)
                pe.wait_ge(s_b, 48)
                for j in range(NT):
                    mm = pe.matmul(k.ps[:, 7, j * NE:j * NE + NE], k.xnT[:, j * P:j * P + P], gw[:], start=True, stop=True)
                T.done(mm, "gate")
                when(pe, V, "cw")
                for i in range(pairs):
                    for u in range(2):
                        when(pe, A, f"cT{u}", i - 1)
                        for t in range(4):
                            mm = pe.transpose(k.ps[0:NE, 4 + u, t * P:t * P + P], cw[:, i * 8 + u * 4 + t, :], k.ident[:])
                        mm.then_inc(T.sem, 1)
                        when(pe, A, f"cT{u}", i)
                        when(pe, V, f"b{u}", i - 1)
                        for t in range(4):
                            mm = pe.matmul(k.ps[:, u, t * P:t * P + P],
                                           cT[:, u, t * P:t * P + P], b2[:], start=True, stop=True)
                        mm.then_inc(T.sem, 1)
                when(pe, V, "b1", pairs - 1)

                def ups(i, s, c, u):
                    n = (i * 2 + s) * NCH + c
                    for f in range(FT):
                        pe.wait_ge(act_.sem, act_.at(n * FT + (f - FT)))
                        pe.matmul(k.ps[:, f, :], w1[:, s, f * P:f * P + P], k.xnT[:, ds(c * CH, CH)],
                                  start=True, stop=True).then_inc(up.sem, 1)

                def downs(i, s, c, u):
                    n = (i * 2 + s) * NCH + c
                    pe.wait_ge(add.sem, add.at(n - 2))
                    for t in range(4):
                        for f in range(FT):
                            if t == 0:
                                pe.wait_ge(act_.sem, act_.at(n * FT + f))
                            mm = pe.matmul(k.ps[:, 4 + u, t * P:t * P + P], h[:, u, f, t * P:t * P + P],
                                           w2[:, s, f, :], start=f == 0, stop=f == FT - 1)
                    mm.then_inc(down.sem, 1)

                def expert(i, s, following):
                    with pe.Fori(0, NCH // 2 - 1) as j:
                        ups(i, s, j * 2 + 1, 1)
                        downs(i, s, j * 2, 0)
                        ups(i, s, j * 2 + 2, 0)
                        downs(i, s, j * 2 + 1, 1)
                    ups(i, s, NCH - 1, 1)
                    downs(i, s, NCH - 2, 0)
                    if following:
                        pe.wait_ge(s_w[1 - s], (following[0] + 1) * 48)
                        ups(*following, 0, 0)
                    downs(i, s, NCH - 1, 1)

                pe.wait_ge(s_w[0], 48)
                ups(0, 0, 0, 0)
                with pe.Fori(0, rounds - 1) as i:
                    expert(i, 0, (i, 1))
                    hold(k, pe)
                    expert(i, 1, (i + 1, 0))
                expert(rounds - 1, 0, (rounds - 1, 1))
                expert(rounds - 1, 1, None)

            @block.scalar
            def _(act):
                act_.seed(act)
                when(act, V, "less")
                A.done(act.activation(pr[:], pr[:], ACT.Exp), "exp")
                act.wait_ge(s_b, 48)
                for i in range(pairs):
                    for u in range(2):
                        when(act, T, f"cT{u}", i)
                        when(act, T, f"b{u}", i - 1)
                        act.copy(cT[:, u, :], k.ps[0:NE, 4 + u, :]).then_inc(A.sem, 1)
                with act.Fori(0, rounds) as i:
                    for s in range(2):
                        act.wait_ge(s_w[s], (i + 1) * 48)
                        hold(k, act)
                        with act.Fori(0, NCH // 2) as j:
                            for u in range(2):
                                n = (i * 2 + s) * NCH + j * 2 + u
                                act.wait_ge(down.sem, down.at(n - 2))
                                for f in range(FT):
                                    act.wait_ge(up.sem, up.at(n * FT + f))
                                    act.activation(h[:, u, f, :], k.ps[:, f, :], ACT.Gelu_apprx_tanh,
                                                   bias=b1[:, s, f:f + 1]).then_inc(act_.sem, 1)

            @block.vector
            def _(dve):
                add.seed(dve)

                def step(ins, name):
                    V.done(ins, name)
                    when(dve, V, name)

                wide = lambda x: x.unsqueeze(2).to_broadcast([P, NT, NE])
                logit = k.ps[:, 7, 0:NT * NE].rearrange("p (t e) -> p t e", e=NE)
                when(dve, T, "gate")
                step(dve.tensor_reduce(den[:], logit, AX_X, ALU.max), "max")
                step(dve.tensor_tensor(pr[:], logit, wide(den[:]), ALU.subtract), "less")
                when(dve, A, "exp")
                step(dve.tensor_reduce(den[:], pr[:], AX_X, ALU.add), "sum")
                step(dve.reciprocal(den[:], den[:]), "rsum")
                step(dve.tensor_tensor(pr[:], pr[:], wide(den[:]), ALU.mult), "prob")
                dve.wait_ge(s_b, 48)
                top2(dve, V, "r", pr[:], work, hot, m, iota[:])
                step(dve.tensor_tensor(den[:], m[:, 0, :], m[:, 1, :], ALU.add), "two")
                step(dve.tensor_scalar(den[:], den[:], 1e-8, None, ALU.add), "eps")
                step(dve.reciprocal(den[:], den[:]), "rden")
                step(dve.tensor_tensor(hot[:, 0], hot[:, 0], hot[:, 1], ALU.add), "hots")
                step(dve.tensor_tensor(pr[:], pr[:], hot[:, 0], ALU.mult), "picked")
                step(dve.tensor_tensor(cw[:], pr[:], wide(den[:]), ALU.mult), "cw")
                for i in range(pairs):
                    for u in range(2):
                        when(dve, T, f"b{u}", i)
                        x = k.x_tm[:, i * 8 + u * 4:i * 8 + u * 4 + 4, :]
                        dve.tensor_tensor(x, x, k.ps[:, u, :].rearrange("p (t d) -> p t d", d=D), ALU.add)\
                           .then_inc(V.sem, 1)
                with dve.Fori(0, rounds) as i:
                    for s in range(2):
                        with dve.Fori(0, NCH // 2) as j:
                            for u in range(2):
                                n = (i * 2 + s) * NCH + j * 2 + u
                                dve.wait_ge(down.sem, down.at(n))
                                dve.wait_ge(add.sem, add.at(n - 1))
                                for t in range(4):
                                    tt = (j * 2 + u) * 4 + t
                                    x = k.x_tm[:, tt, :]
                                    o = dve.scalar_tensor_tensor(
                                        out=x, in0=k.ps[:, 4 + u, t * P:t * P + P],
                                        scalar=cw[:, ds(tt, 1), :].rearrange("p a e -> p (a e)")[:, ds(i * 2 + s, 1)],
                                        in1=x, op0=ALU.mult, op1=ALU.add)
                                o.then_inc(add.sem, 1)


def layer3(k):
    norm_stage(k, "n3", k.x_tm, to_xnT(k))
    with ExitStack() as ctx:
        R = {"qk": k.nc.dram_tensor("qk_parts", (2, NI, 3, HD, GH, S), BF16, kind="Internal").ap(),
             "v": k.sb("l3_v", [P, NI, QT, GH * HD], ctx=ctx), "att": k.sb("l3_att", [P, NI, QT, GH * HD], ctx=ctx)}
        attn3_project_stage(k, R)
        attn3_stage(k, R)
        attn3_out_stage(k, R)
    moe3_stage(k)


def store_stage(k):
    s_out = k.sem("s_out")
    with k.nc.Block() as block:
        @block.sync
        def _(sp):
            sp.dma_start(k.out.rearrange("b (j p) d -> p (b j) d", p=P), k.x_tm[:]).then_inc(s_out, 16)
            sp.wait_ge(s_out, 16)


def constants():
    i = np.arange(P)
    f = np.float32
    return {"ident": np.eye(P, dtype=f), "triu": (i[:, None] <= i[None, :]).astype(f),
            "sel": selectors(), "maskneg": np.where(i[:, None] > i[None, :], f(NEG), f(0)),
            "maskneg_q": np.where(i[:, None] < i[None, :], f(NEG), f(0)),
            "strict": (i[:, None] < i[None, :]).astype(f),
            "shift": (i[:, None] == i[None, :] + 1).astype(f),
            "corner": ((i[:, None] == 0) & (i[None, :] == P - 1)).astype(f),
            "keep": np.repeat((np.arange(NT) % CPB != CPB - 1)[:, None], H2, axis=1).astype(f), "iota": (np.arange(8) - 8).astype(f),
            "head_blocks": (i[:, None] // 8 == i[None, :] // 8).astype(f)}


def layouts(a):
    w = {}
    for d in "fb":
        g = lambda q: a[f"L0a_{d}_{q}"]
        w.update({f"L0a_{d}_inWT": g("inW").T, f"L0a_{d}_convW": g("convW")[:, 0, :].T,
                  f"L0a_{d}_xprojT": g("xprojW").T, f"L0a_{d}_dtWT": g("dtW").T,
                  f"L0a_{d}_outWT": g("outW").T})
        w.update({f"L0a_{d}_{q}": g(q) for q in ("A_log", "convb", "dtb", "Dskip")})
    w["L0a_projWT"] = a["L0a_proj_W"].T
    w["L0f_gateT"], w["L0f_gate_b"] = a["L0f_gate_w"].T, a["L0f_gate_b"]
    w["L0f_expertT"] = a["L0f_expert_w"].transpose(2, 0, 1)
    w["L0f_expert_bT"] = a["L0f_expert_b"].T
    w["L0a_proj_b"] = a["L0a_proj_b"]
    w["L1a_w"] = np.stack([a[f"L1a_w_{q}"] for q in "qkvo"])
    w["L1f_w1T"] = a["L1f_w1"].transpose(2, 0, 1)
    w["L1f_w2T"] = a["L1f_w2"].reshape(8, D, 4, P).transpose(3, 0, 2, 1)
    w["L1f_b1T"] = a["L1f_b1"].reshape(8, 4, P).transpose(2, 0, 1)
    w["L1f_b2"] = a["L1f_b2"]
    w["L2a_winT"], w["L2a_woutT"] = a["L2a_W_in"].T, a["L2a_W_out"].T
    w["L2a_dt_bias"], w["L2a_D_param"] = a["L2a_dt_bias"], a["L2a_D_param"]
    w["L2a_norm_w"] = np.stack([a["L2a_B_norm_w"], a["L2a_C_norm_w"]])
    w["L2a_head_bias"] = np.stack([a["L2a_B_bias"], a["L2a_C_bias"]])
    w["L2f_weightT"], w["L2f_alpha"], w["L2f_bias"] = a["L2f_weight"].T, a["L2f_alpha"], a["L2f_bias"]
    wq = a["L3a_W_qkv"].reshape(D, 16, 3, 8).transpose(0, 2, 1, 3)
    bq = a["L3a_b_qkv"].reshape(16, 3, 8).transpose(1, 0, 2)
    turn = lambda x: x.reshape(*x.shape[:-2], 4, 4, 8).swapaxes(-1, -2).reshape(*x.shape[:-2], D)
    w["L3a_wqkv"] = np.stack([turn(wq[:, 0]), turn(wq[:, 1]), wq[:, 2].reshape(D, D)], axis=1)
    w["L3a_bqkv"] = np.stack([turn(bq[0]), turn(bq[1]), bq[2].reshape(D)])
    w["L3a_wout"], w["L3a_bout"] = a["L3a_W_out"], a["L3a_b_out"]
    w["L3f_routerT"] = a["L3f_router_w"].T
    w["L3f_w1T"] = a["L3f_w1"].transpose(2, 0, 1)
    w["L3f_w2T"] = a["L3f_w2"].reshape(8, D, 4, P).transpose(3, 0, 2, 1)
    w["L3f_b1T"] = a["L3f_b1"].reshape(8, 4, P).transpose(2, 0, 1)
    w["L3f_b2"] = a["L3f_b2"]
    w["L0a_ln"] = np.stack([a["L0a_ln_w"], a["L0a_ln_b"]])
    return w


def layer0(k):
    with ExitStack() as ctx:
        accF = k.sb("accF", [P, TOK], ctx=ctx)
        pad = k.sb("pad", [P, B * ROW], ctx=ctx)
        with ExitStack() as ctx2:
            ln = k.sb("ln", [P, 2], ctx=ctx2)
            xn = k.sb("xn_tm", [P, NT, D], ctx=ctx2)
            s_ln = k.sem("s_ln")
            G = Steps(k, "pool", ["borders"])
            with k.nc.Block() as block:
                @block.sync
                def _(sp):
                    with k.nc.allow_non_contiguous_dma(reason="two columns"):
                        sp.dma_start(ln[:], k.ins["L0a_ln"].rearrange("r p -> p r")).then_inc(s_ln, 16)
                    sp.wait_ge(s_ln, 16)

                @block.gpsimd
                def _(pool):
                    G.done(pool.memset(pad[:], 0.0), "borders")
                    pool.wait_ge(G.sem, G.at("borders"))
            G.close()
            norm_stage(k, "n0", k.x_tm, to_xnT(k), keep=xn)

            def to_pad(act, i, u, bank):
                return act.activation(pad[:, ds(i * ROW + PAD + u * CH, CH)], bank, ACT.Identity,
                                      scale=ln[:, 0:1], bias=ln[:, 1:2])
            norm_stage(k, "n0b", xn, to_pad)
        for d in "fb":
            with ExitStack() as ctx2:
                mamba_stage(k, d, pad, accF, ctx2)
        moe0_stage(k, accF)
        add_back_stage(k, "back0", accF, k.ins["L0a_proj_b"])


def layer1(k):
    norm_stage(k, "n1", k.x_tm, to_xnT(k))
    with ExitStack() as ctx:
        accF = k.sb("acc1", [P, TOK], ctx=ctx)
        attn1_stage(k, accF)
        experts1_stage(k, accF)


def build(nc, ins, out):
    with ExitStack() as ctx:
        k = Kit(nc, ctx, ins, out)
        load_stage(k)
        layer0(k)
        layer1(k)
        layer2(k)
        layer3(k)
        store_stage(k)


def host_arrays(inputs):
    a = {n.replace("_attn_", "a_").replace("_ffn_", "f_"): np.asarray(v) for n, v in inputs.items()}
    t = {"x": a["L0a_x"]}
    return {n: np.ascontiguousarray(v) for n, v in {**t, **layouts(a), **constants()}.items()}


def kernel(**inputs):
    import concourse.bacc as _bacc
    from concourse.bass_utils import run_bass_kernel_spmd as _run

    arrays = host_arrays(inputs)
    nc = _bacc.Bacc("TRN2", target_bir_lowering=False, num_devices=1)
    ins = {n: nc.dram_tensor(f"in_{n}", a.shape, mybir.dt.from_np(a.dtype), kind="ExternalInput").ap()
           for n, a in arrays.items()}
    out = nc.dram_tensor("out", (B, S, D), F32, kind="ExternalOutput").ap()
    build(nc, ins, out)
    r = _run(nc, [{f"in_{n}": a for n, a in arrays.items()}], core_ids=[0])
    return r.results[0]["out"]
```
